# Optimizing a Trainium2 kernel written in Bass

```python
import numpy as np
import jax
import jax.numpy as jnp

def _softmax(x, axis=-1):
    return jax.nn.softmax(x, axis=axis)

def _gelu(x):
    return jax.nn.gelu(x, approximate=True)

def _silu(x):
    return jax.nn.silu(x)

def _sigmoid(x):
    return jax.nn.sigmoid(x)

def _layernorm(x, axis=-1, eps=1e-05):
    m = jnp.mean(x, axis=axis, keepdims=True)
    v = jnp.var(x, axis=axis, keepdims=True)
    return (x - m) / jnp.sqrt(v + eps)

def _scatter_add(tgt, idx, src, axis=0):
    return tgt.at[idx].add(src)

def _segment_sum(src, seg, n):
    return jax.ops.segment_sum(src, seg, n)
kernel_name = 'mk_gnn_preln_d1_gnn_r32_729cb2'

def setup_inputs(seed: int=0):
    np.random.seed(seed)
    _w = jnp.asarray

    def _rec_inputs():
        import jax
        import jax.numpy as jnp
        _gk = jax.random.key(seed)
        x = -1.686e-05 + 1 * jax.random.normal(jax.random.fold_in(_gk, 1), (3125, 160), jnp.float32)
        src = jax.random.randint(jax.random.fold_in(_gk, 2), (50000,), 0, 3125, jnp.int32)
        dst = jnp.minimum((3125 * jax.random.uniform(jax.random.fold_in(_gk, 3), (50000,)) ** 2.0).astype(jnp.int32), 99999)
        _o = jnp.argsort(dst, stable=True)
        src = src[_o]
        dst = dst[_o]
        edge_attr_4 = 0.0007022 + 0.999661 * jax.random.normal(jax.random.fold_in(_gk, 11), (50000, 4), jnp.float32)
        node_vec1 = -0.00915711 + 0.999674 * jax.random.normal(jax.random.fold_in(_gk, 13), (3125, 1), jnp.float32)
        return (x, src, dst, edge_attr_4, node_vec1)
    x, src, dst, edge_attr_4, node_vec1 = _rec_inputs()

    def _L0_gnn_setup():
        import jax, jax.numpy as jnp
        import numpy as np
        MUL0, MUL1 = (64, 32)
        INV_SQRT3 = 1.0 / np.sqrt(3.0)

        def _split(x):
            return (x[:, :MUL0], x[:, MUL0:].reshape(x.shape[0], MUL1, 3))

        def _merge(o0, o1):
            return jnp.concatenate([o0, o1.reshape(o1.shape[0], -1)], axis=-1)

        def _tp(x0, x1, y0, y1, w000, w011, w101, w110):
            fan0 = x0.shape[1] * y0.shape[1] + x1.shape[1] * y1.shape[1]
            fan1 = x0.shape[1] * y1.shape[1] + x1.shape[1] * y0.shape[1]
            out0 = (jnp.einsum('eu,ev,uvw->ew', x0, y0, w000) + INV_SQRT3 * jnp.einsum('euk,evk,uvw->ew', x1, y1, w110)) / np.sqrt(fan0)
            out1 = (jnp.einsum('eu,evk,uvw->ewk', x0, y1, w011) + jnp.einsum('euk,ev,uvw->ewk', x1, y0, w101)) / np.sqrt(fan1)
            return (out0, out1)

        def _lin(x0, x1, w0, w1):
            return (x0 @ w0 / np.sqrt(x0.shape[1]), jnp.einsum('euk,uv->evk', x1, w1) / np.sqrt(x1.shape[1]))
        key = jax.random.key(seed)
        ks = jax.random.split(key, 20)
        N, E = (50000, 15625)
        inp = {'node_features': jax.random.normal(ks[0], (N, MUL0 + 3 * MUL1), dtype=jnp.float32), 'edge_index': jax.random.randint(ks[1], (2, E), 0, N, dtype=jnp.int64), 'edge_attr_tensor': jax.random.normal(ks[2], (E, 4), dtype=jnp.float32), 'node_attr_scalar_raw': jax.random.normal(ks[3], (N, 1), dtype=jnp.float32), 'wm000': jax.random.normal(ks[4], (MUL0, 1, MUL0), dtype=jnp.float32), 'wm011': jax.random.normal(ks[5], (MUL0, 1, MUL1), dtype=jnp.float32), 'wm101': jax.random.normal(ks[6], (MUL1, 1, MUL1), dtype=jnp.float32), 'wm110': jax.random.normal(ks[7], (MUL1, 1, MUL0), dtype=jnp.float32), 'lm0': jax.random.normal(ks[8], (MUL0, MUL0), dtype=jnp.float32), 'lm1': jax.random.normal(ks[9], (MUL1, MUL1), dtype=jnp.float32), 'wu000': jax.random.normal(ks[10], (MUL0, MUL0, MUL0), dtype=jnp.float32), 'wu011': jax.random.normal(ks[11], (MUL0, MUL1, MUL1), dtype=jnp.float32), 'wu101': jax.random.normal(ks[12], (MUL1, MUL0, MUL1), dtype=jnp.float32), 'wu110': jax.random.normal(ks[13], (MUL1, MUL1, MUL0), dtype=jnp.float32), 'lu0': jax.random.normal(ks[14], (MUL0, MUL0), dtype=jnp.float32), 'lu1': jax.random.normal(ks[15], (MUL1, MUL1), dtype=jnp.float32)}
        return inp
    _L0_gnn_all = _L0_gnn_setup()
    _L0_gnn_in = {k: v for k, v in _L0_gnn_all.items() if k in ('wm000', 'wm011', 'wm101', 'wm110', 'lm0', 'lm1', 'wu000', 'wu011', 'wu101', 'wu110', 'lu0', 'lu1')}
    del _L0_gnn_all
    return {'x': x, 'src': src, 'dst': dst, 'edge_attr_4': edge_attr_4, 'node_vec1': node_vec1, 'L0_gnn_wm000': _L0_gnn_in['wm000'], 'L0_gnn_wm011': _L0_gnn_in['wm011'], 'L0_gnn_wm101': _L0_gnn_in['wm101'], 'L0_gnn_wm110': _L0_gnn_in['wm110'], 'L0_gnn_lm0': _L0_gnn_in['lm0'], 'L0_gnn_lm1': _L0_gnn_in['lm1'], 'L0_gnn_wu000': _L0_gnn_in['wu000'], 'L0_gnn_wu011': _L0_gnn_in['wu011'], 'L0_gnn_wu101': _L0_gnn_in['wu101'], 'L0_gnn_wu110': _L0_gnn_in['wu110'], 'L0_gnn_lu0': _L0_gnn_in['lu0'], 'L0_gnn_lu1': _L0_gnn_in['lu1']}

def reference(x, src, dst, edge_attr_4, node_vec1, L0_gnn_wm000, L0_gnn_wm011, L0_gnn_wm101, L0_gnn_wm110, L0_gnn_lm0, L0_gnn_lm1, L0_gnn_wu000, L0_gnn_wu011, L0_gnn_wu101, L0_gnn_wu110, L0_gnn_lu0, L0_gnn_lu1):
    import jax
    import jax.numpy as jnp

    def _L0_gnn_ref(node_features, edge_index, edge_attr_tensor, node_attr_scalar_raw, wm000, wm011, wm101, wm110, lm0, lm1, wu000, wu011, wu101, wu110, lu0, lu1):
        import jax, jax.numpy as jnp
        import numpy as np
        MUL0, MUL1 = (64, 32)
        INV_SQRT3 = 1.0 / np.sqrt(3.0)

        def _split(x):
            return (x[:, :MUL0], x[:, MUL0:].reshape(x.shape[0], MUL1, 3))

        def _merge(o0, o1):
            return jnp.concatenate([o0, o1.reshape(o1.shape[0], -1)], axis=-1)

        def _tp(x0, x1, y0, y1, w000, w011, w101, w110):
            fan0 = x0.shape[1] * y0.shape[1] + x1.shape[1] * y1.shape[1]
            fan1 = x0.shape[1] * y1.shape[1] + x1.shape[1] * y0.shape[1]
            out0 = (jnp.einsum('eu,ev,uvw->ew', x0, y0, w000) + INV_SQRT3 * jnp.einsum('euk,evk,uvw->ew', x1, y1, w110)) / np.sqrt(fan0)
            out1 = (jnp.einsum('eu,evk,uvw->ewk', x0, y1, w011) + jnp.einsum('euk,ev,uvw->ewk', x1, y0, w101)) / np.sqrt(fan1)
            return (out0, out1)

        def _lin(x0, x1, w0, w1):
            return (x0 @ w0 / np.sqrt(x0.shape[1]), jnp.einsum('euk,uv->evk', x1, w1) / np.sqrt(x1.shape[1]))
        N = node_features.shape[0]
        row, col = (edge_index[0], edge_index[1])
        r_vec = edge_attr_tensor[:, :3]
        dist = edge_attr_tensor[:, 3:4]
        e0 = dist
        e1 = r_vec[:, None, :]
        xj0, xj1 = _split(node_features[col])
        m0, m1 = _tp(xj0, xj1, e0, e1, wm000, wm011, wm101, wm110)
        d0, d1 = _lin(xj0, xj1, lm0, lm1)
        msgs = _merge(m0 + d0, m1 + d1)
        agg = jax.ops.segment_sum(msgs, row, num_segments=N)
        a0, a1 = _split(agg)
        x0, x1 = _split(node_features)
        u0, u1 = _tp(x0, x1, a0, a1, wu000, wu011, wu101, wu110)
        ud0, ud1 = _lin(x0, x1, lu0, lu1)
        return node_features + _merge(u0 + ud0, u1 + ud1)
    edge_index = jnp.stack([src, dst])
    h = jnp.maximum(_layernorm(x, axis=-1), 0.0)
    x = x + _L0_gnn_ref(h, edge_index, edge_attr_4, node_vec1, L0_gnn_wm000, L0_gnn_wm011, L0_gnn_wm101, L0_gnn_wm110, L0_gnn_lm0, L0_gnn_lm1, L0_gnn_wu000, L0_gnn_wu011, L0_gnn_wu101, L0_gnn_wu110, L0_gnn_lu0, L0_gnn_lu1)
    return x

_drawn_inputs = setup_inputs


def setup_inputs(seed=0):
    import zlib

    import numpy as np

    out = dict(_drawn_inputs(seed))
    spreads = {}
    factors = {}
    for name, (base, spread) in spreads.items():
        noise = np.random.default_rng([zlib.crc32(name.encode()), seed]).standard_normal(out[name].shape)
        drawn = base * np.exp(spread * noise) if base else spread * noise
        out[name] = jnp.asarray(drawn.astype(out[name].dtype))
    for name, factor in factors.items():
        out[name] = (out[name] * factor).astype(out[name].dtype)
    return out
```

```python
from contextlib import ExitStack

import numpy as np

import concourse.bass as bass
from concourse import mybir


def gnn_layer(nc, x, src, dst, edge_attr, wm000, wm011, wm101, wm110, lm0, lm1,
              wu000, wu011, wu101, wu110, lu0, lu1, out):
    f32, i32 = mybir.dt.float32, mybir.dt.int32
    ALU, ACT, AX = mybir.AluOpType, mybir.ActivationFunctionType, mybir.AxisListType

    N, D = x.shape
    E = src.shape[0]
    M0, M1 = lm0.shape[0], lm1.shape[0]
    V = 3 * M1
    P = 128
    NB = 25
    B = N // NB
    assert B * NB == N and B <= P and M0 + V == D

    EC = -(-E // P)
    TAIL = E - (P - 1) * EC
    assert 0 < TAIL <= EC
    SC = 17
    NSC = EC // SC
    assert NSC * SC == EC
    REC = 6
    GT = 4
    GE = GT * P
    NG = (E - NB) // GE + NB
    NSLOT = 4
    NT = NG * GT
    DUMP = P * NT
    NPAD = P * EC - E
    GH, GD, GR, GV = 0, D, 2 * D, 2 * D + 3 * M0
    GW = GV + M1
    HALF = GW // 2
    NCH = -(-GW // P)
    GREST = GW - (NCH - 1) * P
    MAGIC = 12582912.0
    FAN_M = M0 + M1
    FAN0 = M0 * M0 + M1 * M1
    FAN1 = 2 * M0 * M1
    C3 = 1.0 / np.sqrt(3.0)
    C0 = M0 * M0 // P
    C1 = M1 * M1 // P
    NC = C0 + C1
    TQ = 4
    NQ = NC // TQ
    VP = 16

    h_dram = nc.dram_tensor("h_dram", (N, D), f32, kind="Internal").ap()
    rec_dram = nc.dram_tensor("rec_dram", (P * NT + NPAD, REC), f32, kind="Internal").ap()

    ctx = ExitStack()
    with ctx:
        def sb(name, shape, dt=f32):
            return ctx.enter_context(nc.sbuf_tensor(name, shape, dt))

        def sem(name):
            return ctx.enter_context(nc.semaphore(name))

        h_sb = sb("h_sb", [B, NB, D])
        hx_sb = sb("hx_sb", [B, NB, D])
        G = sb("G", [P, NB, 2, HALF])
        ident = sb("ident", [P, P])
        Wm = sb("Wm", [P, NCH, D])
        W0 = sb("W0", [P, NC, M0])
        W011 = sb("W011", [M0, M1, M1])
        W101 = sb("W101", [M0, M1, M1])
        L0 = sb("L0", [M0, M0])
        L1 = sb("L1", [V, V])
        gblk_i = sb("gblk_i", [P, NG], i32)

        s = {n: sem(n) for n in (
            "nodes_loaded", "edges_loaded", "attrs_loaded", "zero_sent", "weights_loaded", "edge_memset",
            "consts_made", "weights_zeroed", "weights_scaled", "v", "counts_ready", "prefix_ready",
            "rows_ready", "h_ready", "h_stored", "var_ready", "scatters_begun", "std_ready", "staged0", "staged1", "scattered0", "scattered1",
            "sorted", "G_zeroed", "hx_ready")}

        n_weights, loads = [], []
        HB = (NB + 1) // 2
        ZB = -(-NT * REC // GW)
        early = ExitStack()

        def eb(name, shape, dt=f32):
            return early.enter_context(nc.sbuf_tensor(name, shape, dt))
        src_i = eb("src_i", [P, EC], i32)
        dst_i = eb("dst_i", [P, EC], i32)
        ea = eb("ea", [P, EC, 4])
        src_f = eb("src_f", [P, EC])
        blk = eb("blk", [P, EC])
        t1 = eb("t1", [P, EC])
        t2 = eb("t2", [P, EC])
        local = eb("local", [P, EC])
        row_f = eb("row_f", [P, EC])
        lower = eb("lower", [P, P])
        ones = eb("ones", [P, P])
        cnt = eb("cnt", [P, NB + 1])
        small = eb("small", [P, 8, NB + 1])
        gidx = eb("gidx", [P, NG])
        stage = eb("stage", [P, 2, SC, REC])
        stage_row = eb("stage_row", [P, 2, SC], i32)
        mv = eb("mv", [B, 4, NB])

        big = early.enter_context(nc.sbuf_tensor("one_hot_blocks", [P, NB + 1, EC], f32))
        scan = early.enter_context(nc.sbuf_tensor("running_places", [P, HB, EC], f32))
        cps = early.enter_context(nc.psum_tensor("count_prefix", [P, 2, NB + 1], f32))
        with early, nc.Block() as block:

            @block.sync
            def _(sp):
                sp.wait_ge(s["edge_memset"], 3)
                for tile, dram in ((src_i, src), (dst_i, dst)):
                    sp.dma_start(tile[0:P - 1, :], dram[0:(P - 1) * EC].rearrange("(p t) -> p t", t=EC)
                                 ).then_inc(s["edges_loaded"], 16)
                    sp.dma_start(tile[P - 1:P, 0:TAIL], dram[(P - 1) * EC:E].rearrange("(p t) -> p t", p=1)
                                 ).then_inc(s["edges_loaded"], 16)
                sp.dma_start(ea[0:P - 1, :, :], edge_attr[0:(P - 1) * EC, :].rearrange("(p t) c -> p t c", t=EC)
                             ).then_inc(s["attrs_loaded"], 16)
                sp.dma_start(ea[P - 1:P, 0:TAIL, :], edge_attr[(P - 1) * EC:E, :].rearrange("(p t) c -> p t c", p=1)
                             ).then_inc(s["attrs_loaded"], 16)
                sp.dma_start(hx_sb[:, :, :], x.rearrange("(b p) f -> p b f", p=B)).then_inc(s["nodes_loaded"], 16)
                sp.wait_ge(s["consts_made"], 1)
                sp.dma_start(rec_dram[0:P * NT, :].rearrange("(p t) c -> p (t c)", p=P),
                             G[:, 0:ZB, :, :].rearrange("p b i f -> p (b i f)")[:, 0:NT * REC]
                             ).then_inc(s["zero_sent"], 16)
                sp.wait_ge(s["weights_zeroed"], 2)
                wl = s["weights_loaded"]
                def rows(r0, n, c0, w):
                    done = 0
                    while done < n:
                        c, p = divmod(r0 + done, P)
                        m = min(n - done, P - p)
                        sp.dma_start(Wm[p:p + m, c, c0:c0 + w.shape[1]], w[done:done + m, :]).then_inc(wl, 16)
                        done += m
                        loads.append(1)
                pass
                rows(GH, M0, 0, lm0)
                rows(GD, M0, 0, wm000[:, 0, :])
                rows(GV, M1, 0, wm110[:, 0, :])
                for k in range(3):
                    rows(GH + M0 + k * M1, M1, M0 + k * M1, lm1)
                    rows(GD + M0 + k * M1, M1, M0 + k * M1, wm101[:, 0, :])
                    rows(GR + k * M0, M0, M0 + k * M1, wm011[:, 0, :])
                    sp.dma_start(L1[k * M1:(k + 1) * M1, k * M1:(k + 1) * M1], lu1).then_inc(wl, 16)
                sp.dma_start(L0[:, :], lu0).then_inc(wl, 16)
                sp.dma_start(W0[:, 0:C0, :], wu000.rearrange("u v w -> (u v) w").rearrange("(c p) w -> p c w", p=P)
                             ).then_inc(wl, 16)
                sp.dma_start(W0[:, C0:NC, :], wu110.rearrange("u v w -> (u v) w").rearrange("(c p) w -> p c w", p=P)
                             ).then_inc(wl, 16)
                sp.dma_start(W011[:, :, :], wu011).then_inc(wl, 16)
                sp.dma_start(W101[:, :, :], wu101.rearrange("u v w -> v u w")).then_inc(wl, 16)
                n_weights.append(len(loads) + 3 + 5)
                sp.wait_ge(s["h_ready"], 2)
                sp.dma_start(h_dram.rearrange("(b p) f -> p b f", p=B), h_sb[:, :, :]).then_inc(s["h_stored"], 16)
                sp.wait_ge(s["h_stored"], 16)
            
            @block.gpsimd
            def _(pool):
                pool.memset(src_i[96:P, TAIL:EC], N).then_inc(s["edge_memset"], 1)
                pool.memset(dst_i[96:P, TAIL:EC], 0).then_inc(s["edge_memset"], 1)
                pool.memset(ea[96:P, TAIL:EC, :], 0.0).then_inc(s["edge_memset"], 1)
                pool.wait_ge(s["edge_memset"], 3)
                pool.memset(G[:, 0:ZB, :, :], 0.0).then_inc(s["consts_made"], 1)
                pool.memset(ones[:, :], 1.0).then_inc(s["consts_made"], 1)
                pool.memset(lower[:, :], 0.0).then_inc(s["consts_made"], 1)
                pool.memset(ident[:, :], 0.0).then_inc(s["consts_made"], 1)
                pool.wait_ge(s["consts_made"], 4)
                pool.affine_select(out=lower[:, :], in_=lower[:, :], compare_op=ALU.is_ge, fill=1.0,
                                   base=0, pattern=[[-1, P]], channel_multiplier=1).then_inc(s["consts_made"], 1)
                pool.affine_select(out=ident[:, :], in_=ident[:, :], compare_op=ALU.not_equal, fill=1.0,
                                   base=0, pattern=[[-1, P]], channel_multiplier=1).then_inc(s["consts_made"], 1)
                pool.iota(gidx[:, :], pattern=[[1, NG]], base=0, channel_multiplier=0,
                          allow_small_or_imprecise_dtypes=True).then_inc(s["consts_made"], 1)
                pool.wait_ge(s["consts_made"], 7)
                pool.memset(Wm[:, :, :], 0.0).then_inc(s["weights_zeroed"], 1)
                pool.memset(L1[:, :], 0.0).then_inc(s["weights_zeroed"], 1)
                pool.memset(G[:, ZB:NB, :, :], 0.0).then_inc(s["G_zeroed"], 1)
                pool.wait_ge(s["zero_sent"], 16)

                def step(t, slot):
                    pool.wait_ge(s[f"staged{slot}"], 4 * (t // 2 + 1))
                    for j in range(SC):
                        pool.indirect_dma_start(rec_dram, bass.IndirectOffsetOnAxis(ap=stage_row[:, slot, j:j + 1], axis=0),
                                                stage[:, slot, j, :], None).then_inc(s[f"scattered{slot}"], 16)

                with pool.Fori(0, NSC // 2) as i:
                    for slot in range(2):
                        pool.wait_ge(s[f"staged{slot}"], 4 * i + 4)
                        pool.sem_inc(s["scatters_begun"], 1)
                        for j in range(SC):
                            pool.indirect_dma_start(
                                rec_dram, bass.IndirectOffsetOnAxis(ap=stage_row[:, slot, j:j + 1], axis=0),
                                stage[:, slot, j, :], None).then_inc(s[f"scattered{slot}"], 16)
                for t in range(NSC // 2 * 2, NSC):
                    step(t, t % 2)
                pool.wait_ge(s["scattered0"], 16 * SC * ((NSC + 1) // 2))
                pool.wait_ge(s["scattered1"], 16 * SC * (NSC // 2))

            @block.tensor
            def _(pe):
                pe.wait_ge(s["consts_made"], 7)
                pe.wait_ge(s["counts_ready"], 1)
                pe.matmul(cps[:, 0, :], lower[:, :], cnt[:, :], start=True, stop=True)
                pe.matmul(cps[:, 1, :], ones[:, :], cnt[:, :], start=True, stop=True).then_inc(s["prefix_ready"], 1)

            @block.scalar
            def _(act):
                act.wait_ge(s["attrs_loaded"], 32)
                act.wait_ge(s["edges_loaded"], 64)
                act.wait_ge(s["rows_ready"], 1)

                def step(c0, slot, value):
                    act.wait_ge(s[f"scattered{slot}"], value) if value is not None else None
                    cols = bass.ds(c0, SC)
                    act.activation(stage_row[:, slot, :], row_f[:, cols], ACT.Copy).then_inc(s[f"staged{slot}"], 1)
                    act.activation(stage[:, slot, :, 0], local[:, cols], ACT.Copy).then_inc(s[f"staged{slot}"], 1)
                    act.activation(stage[:, slot, :, 1].bitcast(i32), dst_i[:, cols], ACT.Copy
                                   ).then_inc(s[f"staged{slot}"], 1)
                    act.activation(stage[:, slot, :, 2:6], ea[:, cols, :], ACT.Copy).then_inc(s[f"staged{slot}"], 1)

                step(0, 0, None)
                step(SC, 1, None)
                act.wait_ge(s["var_ready"], 1)
                act.activation(mv[:, 3, :], mv[:, 1, :], ACT.Sqrt).then_inc(s["std_ready"], 1)
                act.wait_ge(s["weights_loaded"], 16 * n_weights[0])
                ws = s["weights_scaled"]

                def scaled(ap, c):
                    act.activation(ap, ap, ACT.Copy, scale=float(c)).then_inc(ws, 1)

                def scaled_rows(r0, n, c0, w, c):
                    done = 0
                    while done < n:
                        q, p = divmod(r0 + done, P)
                        m = min(n - done, P - p, P if p == 0 else 2 * M1 if p == 2 * M1 else M1)
                        scaled(Wm[p:p + m, q, c0:c0 + w], c)
                        done += m
                scaled_rows(GH, M0, 0, M0, 1 / np.sqrt(M0))
                scaled_rows(GD, M0, 0, M0, 1 / np.sqrt(FAN_M))
                scaled_rows(GV, M1, 0, M0, C3 / np.sqrt(FAN_M))
                for k in range(3):
                    scaled_rows(GH + M0 + k * M1, M1, M0 + k * M1, M1, 1 / np.sqrt(M1))
                    scaled_rows(GD + M0 + k * M1, M1, M0 + k * M1, M1, 1 / np.sqrt(FAN_M))
                    scaled_rows(GR + k * M0, M0, M0 + k * M1, M1, 1 / np.sqrt(FAN_M))
                scaled(W0[:, 0:C0, :], 1 / np.sqrt(FAN0))
                scaled(W0[:, C0:NC, :], C3 / np.sqrt(FAN0))
                scaled(W011[:, :, :], 1 / np.sqrt(FAN1))
                scaled(W101[:, :, :], 1 / np.sqrt(FAN1))
                scaled(L0[:, :], 1 / np.sqrt(M0))
                scaled(L1[:, :], 1 / np.sqrt(M1))
                with act.Fori(1, NSC // 2) as i:
                    for slot in range(2):
                        step(i * (2 * SC) + slot * SC, slot, i * (16 * SC))
                for t in range(NSC // 2 * 2, NSC):
                    step(t * SC, t % 2, 16 * SC * (t // 2))

            @block.vector
            def _(dve):
                n = [0]

                def link(ins):
                    n[0] += 1
                    ins.then_inc(s["v"], 1)
                    dve.wait_ge(s["v"], n[0])

                dve.wait_ge(s["edges_loaded"], 64)
                link(dve.tensor_copy(src_f[:, :], src_i[:, :]))
                link(dve.tensor_scalar(t1[:, :], src_f[:, :], 1.0 / B, 0.5 / B - 0.5, ALU.mult, ALU.add))
                link(dve.tensor_scalar(t2[:, :], t1[:, :], MAGIC, None, ALU.add))
                link(dve.tensor_scalar(blk[:, :], t2[:, :], -MAGIC, None, ALU.add))
                for b in range(NB + 1):
                    ins = dve.tensor_scalar(big[:, b, :], blk[:, :], float(b), 0.0, ALU.is_equal, ALU.add,
                                            accum_out=cnt[:, b:b + 1])
                    n[0] += 1
                    ins.then_inc(s["v"], 1)
                dve.wait_ge(s["v"], n[0])
                dve.sem_inc(s["counts_ready"], 1)
                link(dve.tensor_scalar(t1[:, :], blk[:, :], -float(B), 1.0, ALU.mult, ALU.add))
                link(dve.tensor_tensor(local[:, :], src_f[:, :], t1[:, :], ALU.add))
                dve.wait_ge(s["prefix_ready"], 1)
                ceil0, ceil1, ngr, incl, first, base = (small[:, i, :] for i in range(6))
                link(dve.tensor_scalar(ceil0, cps[:, 1, :], 1.0 / GE, 0.5 - 0.5 / GE, ALU.mult, ALU.add))
                link(dve.tensor_scalar(ceil1, ceil0, MAGIC, None, ALU.add))
                link(dve.tensor_scalar(ngr, ceil1, -MAGIC, None, ALU.add))
                link(dve.memset(small[:, 6, :], 0.0))
                link(dve.tensor_tensor_scan(incl, ngr, small[:, 6, :], 0.0, ALU.add, ALU.add))
                link(dve.tensor_tensor(first, incl, ngr, ALU.subtract))
                link(dve.memset(first[:, NB:NB + 1], float(NG)))
                link(dve.scalar_tensor_tensor(base, first, float(GE), cps[:, 0, :], ALU.mult, ALU.add))
                for b0 in range(0, NB + 1, HB):
                    for b in range(b0, b0 + HB):
                        ins = dve.tensor_tensor_scan(scan[:, b - b0, :], big[:, b, :], big[:, b, :], base[:, b:b + 1],
                                                     ALU.add, ALU.bypass)
                        n[0] += 1
                        ins.then_inc(s["v"], 1)
                    dve.wait_ge(s["v"], n[0])
                    link(dve.tensor_tensor(big[:, b0:b0 + HB, :], big[:, b0:b0 + HB, :], scan[:, :, :], ALU.mult))
                link(dve.tensor_reduce(t2[:, :], big[:, :, :].rearrange("p b t -> p t b"), AX.X, ALU.add))
                link(dve.tensor_scalar(src_f[:, :], t2[:, :], -1.0, None, ALU.add))
                link(dve.tensor_scalar(t1[:, :], src_f[:, :], 1.0 / P, 0.5 / P - 0.5, ALU.mult, ALU.add))
                link(dve.tensor_scalar(t2[:, :], t1[:, :], MAGIC, None, ALU.add))
                link(dve.tensor_scalar(t1[:, :], t2[:, :], -MAGIC, None, ALU.add))
                link(dve.scalar_tensor_tensor(t2[:, :], t1[:, :], -float(P), src_f[:, :], ALU.mult, ALU.add))
                link(dve.scalar_tensor_tensor(row_f[:, :], t2[:, :], float(NT), t1[:, :], ALU.mult, ALU.add))
                link(dve.tensor_scalar(t1[:, :], blk[:, :], float(NB), None, ALU.is_equal))
                link(dve.tensor_scalar(t2[:, :], src_f[:, :], float(DUMP - NG * GE), None, ALU.add))
                link(dve.tensor_tensor(t2[:, :], t2[:, :], row_f[:, :], ALU.subtract))
                link(dve.tensor_tensor(t2[:, :], t2[:, :], t1[:, :], ALU.mult))
                link(dve.tensor_tensor(row_f[:, :], row_f[:, :], t2[:, :], ALU.add))
                dve.sem_inc(s["rows_ready"], 1)
                gview = scan[:, :, :].rearrange("p b t -> p (b t)")[:, 0:NB * NG].rearrange("p (b g) -> p g b", b=NB)
                dve.wait_ge(s["consts_made"], 7)
                link(dve.tensor_tensor(gview, gidx[:, :].unsqueeze(2).broadcast_to([P, NG, NB]),
                                       incl[:, None, 0:NB].broadcast_to([P, NG, NB]), ALU.is_ge))
                link(dve.tensor_reduce(gidx[:, :], gview, AX.X, ALU.add))
                link(dve.tensor_scalar(gblk_i[:, :], gidx[:, :], float(NB - 1), None, ALU.min))
                dve.wait_ge(s["nodes_loaded"], 16)
                xv = hx_sb[:, :, :]
                xc = big[0:B, :, :].rearrange("p b t -> p (b t)")[:, 0:NB * D].rearrange("p (b f) -> p b f", f=D)
                sq = scan[0:B, :, :].rearrange("p b t -> p (b t)")[:, 0:NB * D].rearrange("p (b f) -> p b f", f=D)

                def each(a):
                    return a.unsqueeze(2).broadcast_to([B, NB, D])
                link(dve.tensor_reduce(mv[:, 0, :], xv, AX.X, ALU.add))
                link(dve.tensor_scalar(mv[:, 0, :], mv[:, 0, :], 1.0 / D, None, ALU.mult))
                link(dve.tensor_tensor(xc, xv, each(mv[:, 0, :]), ALU.subtract))
                link(dve.tensor_tensor(sq, xc, xc, ALU.mult))
                link(dve.tensor_reduce(mv[:, 1, :], sq, AX.X, ALU.add))
                link(dve.tensor_scalar(mv[:, 1, :], mv[:, 1, :], 1.0 / D, 1e-5, ALU.mult, ALU.add))
                dve.sem_inc(s["var_ready"], 1)
                dve.wait_ge(s["std_ready"], 1)
                link(dve.reciprocal(mv[:, 2, :], mv[:, 3, :]))
                link(dve.tensor_tensor(sq, xc, each(mv[:, 2, :]), ALU.mult))
                link(dve.tensor_scalar(xc, sq, 0.0, None, ALU.max))
                dve.tensor_copy(h_sb[:, :, 0:M0], xc[:, :, 0:M0]).then_inc(s["h_ready"], 1)
                dve.tensor_copy(h_sb[:, :, M0:D].rearrange("p b (k u) -> p b u k", k=3),
                                xc[:, :, M0:D].rearrange("p b (u k) -> p b u k", k=3)).then_inc(s["h_ready"], 1)
                link(dve.tensor_tensor(hx_sb[:, :, :], xv, xc, ALU.add))

        sums = ExitStack()
        rec = sums.enter_context(nc.sbuf_tensor("rec", [P, NSLOT, GT, REC], f32))
        Z = sums.enter_context(nc.sbuf_tensor("Z", [P, NSLOT, GT, GW], f32))
        O = sums.enter_context(nc.sbuf_tensor("O", [P, NSLOT, GT, B], f32))
        rv = sums.enter_context(nc.sbuf_tensor("rv", [P, 2, GT, 3, M1], f32))
        rs = sums.enter_context(nc.sbuf_tensor("rs", [P, 2, GT, M1], f32))
        nodes = sums.enter_context(nc.sbuf_tensor("node_numbers", [P, B], f32))
        gp = sums.enter_context(nc.psum_tensor("G_part", [P, 2, 2, 512], f32))
        q = {n: sem(n) for n in (
            "numbers_made", "rec_free", "z_free", "G_added", "ps_free", "products", "dist_products", "G_part_ready",
            "rv_step", "gathers_begun")}
        rec_in = [sem(f"rec_in{i}") for i in range(NSLOT)]
        gathered = [sem(f"gathered{i}") for i in range(NSLOT)]
        NDVE = 6
        LOOPS, LEFT = divmod(NG, NSLOT)
        rec_rows = rec_dram[0:P * NT, :].rearrange("(p t) c -> p t c", p=P)

        def groups(eng, body):
            with eng.Fori(0, LOOPS) as i:
                for slot in range(NSLOT):
                    body(i * NSLOT + slot, i, slot)
            for slot in range(LEFT):
                body(LOOPS * NSLOT + slot, LOOPS, slot)

        with sums, nc.Block() as block:

            @block.sync
            def _(sp):
                def load(g, turn, slot):
                    sp.wait_ge(q["rec_free"], g + 1)
                    sp.dma_start(rec[:, slot, :, :], rec_rows[:, bass.ds(g * GT, GT), :]).then_inc(rec_in[slot], 16)
                groups(sp, load)

            @block.gpsimd
            def _(pool):
                pool.iota(nodes[:, :], pattern=[[1, B]], base=1, channel_multiplier=0,
                          allow_small_or_imprecise_dtypes=True).then_inc(q["numbers_made"], 1)

                def gather(g, turn, slot):
                    pool.wait_ge(q["z_free"], g + 1)
                    pool.wait_ge(rec_in[slot], turn * 16 + 16)
                    pool.sem_inc(q["gathers_begun"], 1)
                    for j in range(GT):
                        pool.indirect_dma_start(
                            Z[:, slot, j, 0:D], None, h_dram,
                            bass.IndirectOffsetOnAxis(ap=rec[:, slot, j, 1:2].bitcast(i32), axis=0)
                        ).then_inc(gathered[slot], 16)
                groups(pool, gather)

            @block.scalar
            def _(act):
                def dist(g, turn, slot):
                    act.wait_ge(gathered[slot], turn * (16 * GT) + 16 * GT)
                    for j in range(GT):
                        act.activation(Z[:, slot, j, GD:GD + D], Z[:, slot, j, GH:GH + D], ACT.Copy,
                                       scale=rec[:, slot, j, 5:6]).then_inc(q["dist_products"], 1)
                groups(act, dist)

            @block.tensor
            def _(pe):
                pe.sem_inc(q["z_free"], NSLOT)

                def product(g, turn, slot):
                    pe.wait_ge(q["products"], 3 * g + 3)
                    pe.wait_ge(q["dist_products"], GT * g + GT)
                    pe.wait_ge(q["ps_free"], g + 1)
                    half_bank = slot % 2
                    for j in range(GT):
                        for i in range(2):
                            last = pe.matmul(gp[0:B, half_bank, i, 0:HALF], O[:, slot, j, :],
                                             Z[:, slot, j, i * HALF:(i + 1) * HALF], start=j == 0, stop=j == GT - 1)
                            if j == GT - 1:
                                last.then_inc(q["G_part_ready"], 1)
                    
                    pe.wait_ge(q["G_part_ready"], 2 * g + 2)
                    pe.sem_inc(q["z_free"], 1)
                groups(pe, product)

            @block.vector
            def _(dve):
                dve.sem_inc(q["rec_free"], NSLOT)
                dve.sem_inc(q["ps_free"], 2)
                dve.wait_ge(q["numbers_made"], 1)
                r = [None]

                def add(g, slot):
                    at = r[0][slot]
                    dve.wait_ge(q["G_part_ready"], 2 * g + 2)
                    dve.wait_ge(q["G_added"], g + 1)
                    dve.tensor_tensor(G[0:B, bass.ds(at, 1), :, :], G[0:B, bass.ds(at, 1), :, :],
                                      gp[0:B, slot % 2:slot % 2 + 1, :, 0:HALF], ALU.add).then_inc(q["G_added"], 1)
                    dve.wait_ge(q["G_added"], g + 2)
                    dve.sem_inc(q["ps_free"], 1)

                def step(g, turn, slot):
                    if slot == 0:
                        k = NSLOT if not isinstance(g, int) else LEFT
                        r[0] = [dve.value_load(gblk_i[0:1, bass.ds(g + m, 1)], min_val=0, max_val=NB - 1) for m in range(k)]
                    c = rec[:, slot, :, :]
                    zs = Z[:, slot, :, :]
                    h = slot % 2
                    dve.wait_ge(rec_in[slot], turn * 16 + 16)
                    dve.wait_ge(q["z_free"], g + 1)
                    dve.tensor_tensor(O[:, slot, :, :], nodes[:, None, :].broadcast_to([P, GT, B]),
                                      c[:, :, 0:1].broadcast_to([P, GT, B]), ALU.is_equal).then_inc(q["products"], 1)
                    dve.wait_ge(gathered[slot], turn * (16 * GT) + 16 * GT)
                    dve.tensor_tensor(rv[:, h, :, :, :], zs[:, :, M0:D].rearrange("p j (k u) -> p j k u", k=3),
                                      c[:, :, 2:5].unsqueeze(3).broadcast_to([P, GT, 3, M1]), ALU.mult
                                      ).then_inc(q["rv_step"], 1)
                    dve.tensor_tensor(zs[:, :, GR:GV].rearrange("p j (k u) -> p j k u", k=3),
                                      zs[:, :, None, 0:M0].broadcast_to([P, GT, 3, M0]),
                                      c[:, :, 2:5].unsqueeze(3).broadcast_to([P, GT, 3, M0]), ALU.mult
                                      ).then_inc(q["products"], 1)
                    dve.wait_ge(q["rv_step"], 2 * g + 1)
                    dve.tensor_tensor(rs[:, h, :, :], rv[:, h, :, 0, :], rv[:, h, :, 1, :], ALU.add
                                      ).then_inc(q["rv_step"], 1)
                    dve.wait_ge(q["rv_step"], 2 * g + 2)
                    dve.tensor_tensor(zs[:, :, GV:GW], rs[:, h, :, :], rv[:, h, :, 2, :], ALU.add
                                      ).then_inc(q["products"], 1)
                    add(g, slot)
                    dve.wait_ge(q["dist_products"], GT * g + GT)
                    dve.sem_inc(q["rec_free"], 1)
                dve.sem_inc(q["G_added"], 1)
                groups(dve, step)

        up = ExitStack()

        def ub(name, shape):
            return up.enter_context(nc.sbuf_tensor(name, shape, f32))
        Gs = ub("Gs", [B, 2, GW])
        hs = ub("hs", [B, 2, D])
        GT_ = ub("GT", [P, 2, NCH, B])
        h0T = ub("h0T", [M0, 2, B])
        h1T = ub("h1T", [V, 2, B])
        a_sb = ub("agg", [B, 2, D])
        a0T = ub("a0T", [M0, 2, B])
        C = ub("C", [B, 2, 3, 2 * M1])
        pairs = ub("pairs", [B, 2, NC * P])
        q3 = ub("q3", [B, 3, M1 * M1])
        PT = ub("PT", [P, 2, TQ, B])
        prod = ub("prod", [B, 3, 2 * M1, M1])
        vsum = ub("vsum", [B, 2, 3, M1])
        o1 = ub("o1", [B, 2, V])
        res = ub("res", [B, 2, D])
        psA = up.enter_context(nc.psum_tensor("psA", [P, 512], f32))
        psO = up.enter_context(nc.psum_tensor("psO", [P, 512], f32))
        psT = up.enter_context(nc.psum_tensor("psT", [P, 4, 512], f32))
        psP = up.enter_context(nc.psum_tensor("psP", [P, 2, 512], f32))
        u = {n: sem(n) for n in (
            "block_staged", "staged_free", "trA", "evacA", "C_ready", "T_ready", "T_free",
            "pairs_v", "pairs_p", "p_step", "chunks_tr", "chunks_out", "pt_free", "O_ready", "O_free",
            "prod_done", "vsum_done", "o1_done", "res_done", "store_free", "a_transposes_begun")}
        stored = [sem("stored0"), sem("stored1")]


        def blocks(eng, body):
            with eng.Fori(0, NB // 2) as i:
                for slot in range(2):
                    body(i * 2 + slot, i, slot)
            for b in range(NB // 2 * 2, NB):
                body(b, NB // 2, b % 2)
        out_v = out.rearrange("(b p) f -> p b f", p=B)

        with up, nc.Block() as block:

            @block.scalar
            def _(act):
                act.sem_inc(u["evacA"], 1)
                act.sem_inc(u["chunks_out"], 2)

                def step(b, turn, slot):
                    act.wait_ge(u["staged_free"], b + 1)
                    act.activation(Gs[:, slot, :], G[0:B, bass.ds(b, 1), :, :].rearrange("p b i f -> p (b i f)"),
                                   ACT.Copy).then_inc(u["block_staged"], 1)
                    act.activation(hs[:, slot, :], h_sb[:, bass.ds(b, 1), :].rearrange("p b f -> p (b f)"),
                                   ACT.Copy).then_inc(u["block_staged"], 1)
                    act.wait_ge(u["trA"], 4 * b + 1)
                    act.activation(GT_[:, slot, 0:4, :], psA[:, 0:4 * B].rearrange("p (c n) -> p c n", c=4), ACT.Copy
                                   ).then_inc(u["evacA"], 1)
                    act.wait_ge(u["trA"], 4 * b + 2)
                    act.activation(GT_[0:GREST, slot, 4, :], psA[0:GREST, 0:B], ACT.Copy).then_inc(u["evacA"], 1)
                    act.activation(h0T[:, slot, :], psA[0:M0, B:2 * B], ACT.Copy).then_inc(u["evacA"], 1)
                    act.activation(h1T[:, slot, :], psA[0:V, 2 * B:3 * B], ACT.Copy).then_inc(u["evacA"], 1)
                    act.wait_ge(u["trA"], 4 * b + 3)
                    act.activation(a_sb[:, slot, :], psA[0:B, 0:D], ACT.Copy).then_inc(u["evacA"], 1)
                    act.activation(C[:, slot, :, 0:M1], psA[0:B, M0:D].rearrange("p (k u) -> p k u", k=3), ACT.Copy
                                   ).then_inc(u["evacA"], 1)
                    act.activation(C[:, slot, :, M1:2 * M1], hs[:, slot, M0:D].rearrange("p (k u) -> p k u", k=3),
                                   ACT.Copy).then_inc(u["evacA"], 1)
                    act.wait_ge(u["trA"], 4 * b + 4)
                    act.activation(a0T[:, slot, :], psA[0:M0, 0:B], ACT.Copy).then_inc(u["evacA"], 1)
                    for c in range(NQ):
                        act.wait_ge(u["chunks_tr"], b * NQ + c + 1)
                        act.wait_ge(u["pt_free"], b * NQ + c + 1)
                        act.activation(PT[:, c % 2, :, :], psP[:, c % 2, 0:TQ * B].rearrange("p (c n) -> p c n", c=TQ),
                                       ACT.Copy).then_inc(u["chunks_out"], 1)
                blocks(act, step)

            NEV = 8

            @block.tensor
            def _(pe):
                pe.sem_inc(u["staged_free"], 2)
                pe.sem_inc(u["pt_free"], 2)

                def step(b, turn, slot):
                    idn = ident[0:B, 0:B]
                    pe.wait_ge(u["block_staged"], 2 * b + 2)
                    pe.wait_ge(u["evacA"], NEV * b + 1)
                    for c in range(4):
                        last = pe.transpose(psA[:, c * B:(c + 1) * B], Gs[:, slot, c * P:(c + 1) * P], idn)
                    last.then_inc(u["trA"], 1)
                    pe.wait_ge(u["evacA"], NEV * b + 2)
                    pe.transpose(psA[0:GREST, 0:B], Gs[:, slot, 4 * P:GW], idn)
                    pe.transpose(psA[0:M0, B:2 * B], hs[:, slot, 0:M0], idn)
                    pe.transpose(psA[0:V, 2 * B:3 * B], hs[:, slot, M0:D], idn).then_inc(u["trA"], 1)
                    pe.wait_ge(u["evacA"], NEV * b + 5)
                    for c in range(NCH):
                        k = P if c < NCH - 1 else GREST
                        last = pe.matmul(psA[0:B, 0:D], GT_[0:k, slot, c, :], Wm[0:k, c, :],
                                         start=c == 0, stop=c == NCH - 1)
                    last.then_inc(u["trA"], 1)
                    pe.wait_ge(u["evacA"], NEV * b + 8)
                    pe.sem_inc(u["a_transposes_begun"], 1)
                    pe.transpose(psA[0:M0, 0:B], a_sb[:, slot, 0:M0], idn).then_inc(u["trA"], 1)
                    pe.wait_ge(u["T_free"], b + 1)
                    for i in range(2):
                        pe.matmul(psT[0:B, i, :], h0T[:, slot, :], W011[:, i * 16:(i + 1) * 16, :].rearrange("p v w -> p (v w)"),
                                  start=True, stop=True)
                    pe.wait_ge(u["evacA"], NEV * b + 9)
                    for i in range(2):
                        last = pe.matmul(psT[0:B, 2 + i, :], a0T[:, slot, :],
                                         W101[:, i * 16:(i + 1) * 16, :].rearrange("p v w -> p (v w)"), start=True, stop=True)
                    last.then_inc(u["T_ready"], 1)
                    pe.wait_ge(u["O_free"], b + 1)
                    pe.matmul(psO[0:B, M0:D], h1T[:, slot, :], L1[:, :], start=True, stop=True)
                    pe.matmul(psO[0:B, 0:M0], h0T[:, slot, :], L0[:, :], start=True, stop=False)
                    for c in range(NQ + 1):
                        if c < NQ:
                            if c == 0:
                                pe.wait_ge(u["pairs_v"], b + 1)
                                pe.wait_ge(u["pairs_p"], 2 * b + 3)
                            pe.wait_ge(u["chunks_out"], b * NQ + c + 1)
                            for m in range(TQ):
                                ch = c * TQ + m
                                last = pe.transpose(psP[:, c % 2, m * B:(m + 1) * B],
                                                    pairs[:, slot, ch * P:(ch + 1) * P], idn)
                            last.then_inc(u["chunks_tr"], 1)
                        if c > 0:
                            e = c - 1
                            pe.wait_ge(u["chunks_out"], b * NQ + e + 3)
                            for m in range(TQ):
                                ch = e * TQ + m
                                last = pe.matmul(psO[0:B, 0:M0], PT[:, e % 2, m, :], W0[:, ch, :],
                                                 start=False, stop=ch == NC - 1)
                            last.then_inc(u["pt_free"], 1)
                    pe.wait_ge(u["pt_free"], b * NQ + NQ + 2)
                    pe.sem_inc(u["O_ready"], 1)
                    pe.sem_inc(u["staged_free"], 1)
                blocks(pe, step)

            @block.gpsimd
            def _(pool):
                pool.sem_inc(u["pairs_p"], 1)

                def step(b, turn, slot):
                    pool.wait_ge(u["evacA"], NEV * b + 8)
                    pool.wait_ge(u["staged_free"], b + 1)
                    a, h = a_sb[:, slot, :], hs[:, slot, :]
                    pool.wait_ge(u["pairs_p"], 2 * b + 1)
                    for k in range(3):
                        lo = M0 + k * M1
                        pool.tensor_tensor(q3[:, k, :].rearrange("p (u v) -> p u v", v=M1),
                                           h[:, lo:lo + M1].unsqueeze(2).broadcast_to([B, M1, M1]),
                                           a[:, None, lo:lo + M1].broadcast_to([B, M1, M1]), ALU.mult
                                           ).then_inc(u["p_step"], 1)
                    dst = pairs[:, slot, C0 * P:NC * P]
                    pool.wait_ge(u["p_step"], 4 * b + 3)
                    pool.tensor_tensor(q3[:, 0, :], q3[:, 0, :], q3[:, 1, :], ALU.add
                                       ).then_inc(u["p_step"], 1)
                    pool.wait_ge(u["p_step"], 4 * b + 4)
                    pool.tensor_tensor(dst, q3[:, 0, :], q3[:, 2, :], ALU.add).then_inc(u["pairs_p"], 1)
                    pool.tensor_tensor(pairs[:, slot, (M0 - VP) * M0:M0 * M0].rearrange("p (u v) -> p u v", v=M0),
                                       h[:, M0 - VP:M0].unsqueeze(2).broadcast_to([B, VP, M0]),
                                       a[:, None, 0:M0].broadcast_to([B, VP, M0]), ALU.mult
                                       ).then_inc(u["pairs_p"], 1)
                blocks(pool, step)

            @block.vector
            def _(dve):
                dve.sem_inc(u["T_free"], 1)
                dve.sem_inc(u["O_free"], 1)

                def finish(b, slot):
                    at = bass.ds(b, 1)
                    dve.wait_ge(u["O_ready"], b + 1)
                    o = res[:, slot, :]
                    dve.tensor_tensor(o1[:, slot, :], psO[0:B, M0:D], vsum[:, slot, :, :].rearrange("p k w -> p (k w)"),
                                      ALU.add).then_inc(u["o1_done"], 1)
                    dve.tensor_tensor(o[:, None, 0:M0], psO[0:B, None, 0:M0], hx_sb[:, at, 0:M0], ALU.add
                                      ).then_inc(u["res_done"], 1)
                    dve.wait_ge(u["o1_done"], b + 1)
                    dve.tensor_tensor(o[:, None, M0:D].rearrange("p b (u k) -> p b u k", k=3),
                                      o1[:, slot, None, :].rearrange("p b (k u) -> p b u k", k=3),
                                      hx_sb[:, at, M0:D].rearrange("p b (u k) -> p b u k", k=3), ALU.add
                                      ).then_inc(u["res_done"], 1)
                    dve.wait_ge(u["res_done"], 2 * b + 2)
                    dve.sem_inc(u["O_free"], 1)

                def step(b, turn, slot):
                    dve.wait_ge(u["evacA"], NEV * b + 8)
                    dve.wait_ge(u["staged_free"], b + 1)
                    a, h = a_sb[:, slot, :], hs[:, slot, :]
                    dve.tensor_tensor(pairs[:, slot, 0:(M0 - VP) * M0].rearrange("p (u v) -> p u v", v=M0),
                                      h[:, 0:M0 - VP].unsqueeze(2).broadcast_to([B, M0 - VP, M0]),
                                      a[:, None, 0:M0].broadcast_to([B, M0 - VP, M0]), ALU.mult
                                      ).then_inc(u["pairs_v"], 1)
                    dve.wait_ge(u["T_ready"], b + 1)
                    for k in range(3):
                        last = dve.tensor_tensor(
                            prod[:, k, :, :], psT[0:B, :, :].rearrange("p i (c w) -> p (i c) w", w=M1),
                            C[:, slot, k, :].unsqueeze(2).broadcast_to([B, 2 * M1, M1]), ALU.mult)
                        last.then_inc(u["prod_done"], 1)
                    dve.wait_ge(u["prod_done"], 3 * b + 3)
                    dve.sem_inc(u["T_free"], 1)
                    dve.tensor_reduce(vsum[:, slot, :, :], prod[:, :, :, :].rearrange("p k c w -> p k w c"), AX.X, ALU.add
                                      ).then_inc(u["vsum_done"], 1)
                    dve.wait_ge(u["vsum_done"], b + 1)
                    dve.wait_ge(u["store_free"], b + 1)
                    finish(b, slot)
                blocks(dve, step)

            @block.sync
            def _(sp):
                def store(b, turn, slot):
                    sp.wait_ge(u["res_done"], 2 * b + 2)
                    sp.dma_start(out_v[:, bass.ds(b, 1), :], res[:, slot, None, :]).then_inc(stored[slot], 16)
                    sp.wait_ge(stored[slot], turn * 16 + 16)
                    sp.sem_inc(u["store_free"], 1)
                sp.sem_inc(u["store_free"], 2)
                blocks(sp, store)
                sp.wait_ge(stored[0], 16 * ((NB + 1) // 2))
                sp.wait_ge(stored[1], 16 * (NB // 2))


_INS = ["x", "src", "dst", "edge_attr_4"] + ["L0_gnn_" + n for n in (
    "wm000", "wm011", "wm101", "wm110", "lm0", "lm1", "wu000", "wu011", "wu101", "wu110", "lu0", "lu1")]


def kernel(**inputs):
    import concourse.bacc as _bacc
    from concourse.bass_utils import run_bass_kernel_spmd as _run

    nc = _bacc.Bacc("TRN2", target_bir_lowering=False, num_devices=1)
    arrays, args = {}, []
    for name in _INS:
        a = np.ascontiguousarray(inputs[name])
        arrays[f"in_{name}"] = a
        args.append(nc.dram_tensor(f"in_{name}", a.shape, mybir.dt.from_np(a.dtype), kind="ExternalInput").ap())
    shape = arrays["in_x"].shape
    args.append(nc.dram_tensor("out", shape, mybir.dt.float32, kind="ExternalOutput").ap())
    gnn_layer(nc, *args)
    r = _run(nc, [arrays], core_ids=[0])
    return r.results[0]["out"]
```

```python
from contextlib import ExitStack

import numpy as np

import concourse.bass as bass
from concourse import mybir


def gnn_layer(nc, x, src, dst, edge_attr, wm000, wm011, wm101, wm110, lm0, lm1,
              wu000, wu011, wu101, wu110, lu0, lu1, out):
    f32, i32 = mybir.dt.float32, mybir.dt.int32
    ALU, ACT, AX = mybir.AluOpType, mybir.ActivationFunctionType, mybir.AxisListType

    N, D = x.shape
    E = src.shape[0]
    M0, M1 = lm0.shape[0], lm1.shape[0]
    V = 3 * M1
    P = 128
    NB = 25
    B = N // NB
    assert B * NB == N and B <= P and M0 + V == D

    EC = -(-E // P)
    TAIL = E - (P - 1) * EC
    assert 0 < TAIL <= EC
    SC = 17
    NSC = EC // SC
    assert NSC * SC == EC
    REC = 6
    GT = 3
    GE = GT * P
    NG = (E - NB) // GE + NB
    NSLOT = 4
    NT = NG * GT
    DUMP = P * NT
    NPAD = P * EC - E
    GH, GD, GR, GV = 0, D, 2 * D, 2 * D + 3 * M0
    GW = GV + M1
    HALF = GW // 2
    NCH = -(-GW // P)
    GREST = GW - (NCH - 1) * P
    MAGIC = 12582912.0
    FAN_M = M0 + M1
    FAN0 = M0 * M0 + M1 * M1
    FAN1 = 2 * M0 * M1
    C3 = 1.0 / np.sqrt(3.0)
    C0 = M0 * M0 // P
    C1 = M1 * M1 // P
    NC = C0 + C1
    TQ = 4
    NQ = NC // TQ
    VP = 16
    VA = 15

    h_dram = nc.dram_tensor("h_dram", (N, D), f32, kind="Internal").ap()
    rec_dram = nc.dram_tensor("rec_dram", (P * NT + NPAD, REC), f32, kind="Internal").ap()

    ctx = ExitStack()
    with ctx:
        def sb(name, shape, dt=f32):
            return ctx.enter_context(nc.sbuf_tensor(name, shape, dt))

        def sem(name):
            return ctx.enter_context(nc.semaphore(name))

        h_sb = sb("h_sb", [B, NB, D])
        hx_sb = sb("hx_sb", [B, NB, D])
        G = sb("G", [P, NB, 2, HALF])
        ident = sb("ident", [P, P])
        Wm = sb("Wm", [P, NCH, D])
        W0 = sb("W0", [P, NC, M0])
        W011 = sb("W011", [M0, M1, M1])
        W101 = sb("W101", [M0, M1, M1])
        L0 = sb("L0", [M0, M0])
        L1 = sb("L1", [V, V])
        gblk_i = sb("gblk_i", [P, NG], i32)

        s = {n: sem(n) for n in (
            "nodes_loaded", "edges_loaded", "attrs_loaded", "zero_sent", "weights_loaded", "edge_memset",
            "consts_made", "weights_zeroed", "weights_scaled", "v", "counts_ready", "prefix_ready",
            "rows_ready", "h_ready", "h_stored", "var_ready", "scatters_begun", "std_ready", "staged0", "staged1", "scattered0", "scattered1",
            "sorted", "G_zeroed", "hx_ready")}

        n_weights, loads = [], []
        HB = (NB + 1) // 2
        ZB = -(-NT * REC // GW)
        early = ExitStack()

        def eb(name, shape, dt=f32):
            return early.enter_context(nc.sbuf_tensor(name, shape, dt))
        src_i = eb("src_i", [P, EC], i32)
        dst_i = eb("dst_i", [P, EC], i32)
        ea = eb("ea", [P, EC, 4])
        src_f = eb("src_f", [P, EC])
        blk = eb("blk", [P, EC])
        t1 = eb("t1", [P, EC])
        t2 = eb("t2", [P, EC])
        local = eb("local", [P, EC])
        row_f = eb("row_f", [P, EC])
        lower = eb("lower", [P, P])
        ones = eb("ones", [P, P])
        cnt = eb("cnt", [P, NB + 1])
        small = eb("small", [P, 8, NB + 1])
        gidx = eb("gidx", [P, NG])
        stage = eb("stage", [P, 2, SC, REC])
        stage_row = eb("stage_row", [P, 2, SC], i32)
        mv = eb("mv", [B, 4, NB])

        big = early.enter_context(nc.sbuf_tensor("one_hot_blocks", [P, NB + 1, EC], f32))
        scan = early.enter_context(nc.sbuf_tensor("running_places", [P, HB, EC], f32))
        cps = early.enter_context(nc.psum_tensor("count_prefix", [P, 2, NB + 1], f32))
        with early, nc.Block() as block:

            @block.sync
            def _(sp):
                sp.wait_ge(s["edge_memset"], 3)
                for tile, dram in ((src_i, src), (dst_i, dst)):
                    sp.dma_start(tile[0:P - 1, :], dram[0:(P - 1) * EC].rearrange("(p t) -> p t", t=EC)
                                 ).then_inc(s["edges_loaded"], 16)
                    sp.dma_start(tile[P - 1:P, 0:TAIL], dram[(P - 1) * EC:E].rearrange("(p t) -> p t", p=1)
                                 ).then_inc(s["edges_loaded"], 16)
                sp.dma_start(ea[0:P - 1, :, :], edge_attr[0:(P - 1) * EC, :].rearrange("(p t) c -> p t c", t=EC)
                             ).then_inc(s["attrs_loaded"], 16)
                sp.dma_start(ea[P - 1:P, 0:TAIL, :], edge_attr[(P - 1) * EC:E, :].rearrange("(p t) c -> p t c", p=1)
                             ).then_inc(s["attrs_loaded"], 16)
                sp.dma_start(hx_sb[:, :, :], x.rearrange("(b p) f -> p b f", p=B)).then_inc(s["nodes_loaded"], 16)
                sp.wait_ge(s["consts_made"], 1)
                sp.dma_start(rec_dram[0:P * NT, :].rearrange("(p t) c -> p (t c)", p=P),
                             G[:, 0:ZB, :, :].rearrange("p b i f -> p (b i f)")[:, 0:NT * REC]
                             ).then_inc(s["zero_sent"], 16)
                sp.wait_ge(s["weights_zeroed"], 2)
                wl = s["weights_loaded"]
                def rows(r0, n, c0, w):
                    done = 0
                    while done < n:
                        c, p = divmod(r0 + done, P)
                        m = min(n - done, P - p)
                        sp.dma_start(Wm[p:p + m, c, c0:c0 + w.shape[1]], w[done:done + m, :]).then_inc(wl, 16)
                        done += m
                        loads.append(1)
                pass
                rows(GH, M0, 0, lm0)
                rows(GD, M0, 0, wm000[:, 0, :])
                rows(GV, M1, 0, wm110[:, 0, :])
                for k in range(3):
                    rows(GH + M0 + k * M1, M1, M0 + k * M1, lm1)
                    rows(GD + M0 + k * M1, M1, M0 + k * M1, wm101[:, 0, :])
                    rows(GR + k * M0, M0, M0 + k * M1, wm011[:, 0, :])
                    sp.dma_start(L1[k * M1:(k + 1) * M1, k * M1:(k + 1) * M1], lu1).then_inc(wl, 16)
                sp.dma_start(L0[:, :], lu0).then_inc(wl, 16)
                sp.dma_start(W0[:, 0:C0, :], wu000.rearrange("u v w -> (u v) w").rearrange("(c p) w -> p c w", p=P)
                             ).then_inc(wl, 16)
                sp.dma_start(W0[:, C0:NC, :], wu110.rearrange("u v w -> (u v) w").rearrange("(c p) w -> p c w", p=P)
                             ).then_inc(wl, 16)
                sp.dma_start(W011[:, :, :], wu011).then_inc(wl, 16)
                sp.dma_start(W101[:, :, :], wu101.rearrange("u v w -> v u w")).then_inc(wl, 16)
                n_weights.append(len(loads) + 3 + 5)
                sp.wait_ge(s["h_ready"], 2)
                sp.dma_start(h_dram.rearrange("(b p) f -> p b f", p=B), h_sb[:, :, :]).then_inc(s["h_stored"], 16)
                sp.wait_ge(s["h_stored"], 16)
            
            @block.gpsimd
            def _(pool):
                pool.memset(src_i[96:P, TAIL:EC], N).then_inc(s["edge_memset"], 1)
                pool.memset(dst_i[96:P, TAIL:EC], 0).then_inc(s["edge_memset"], 1)
                pool.memset(ea[96:P, TAIL:EC, :], 0.0).then_inc(s["edge_memset"], 1)
                pool.wait_ge(s["edge_memset"], 3)
                pool.memset(G[:, 0:ZB, :, :], 0.0).then_inc(s["consts_made"], 1)
                pool.memset(ones[:, :], 1.0).then_inc(s["consts_made"], 1)
                pool.memset(lower[:, :], 0.0).then_inc(s["consts_made"], 1)
                pool.memset(ident[:, :], 0.0).then_inc(s["consts_made"], 1)
                pool.wait_ge(s["consts_made"], 4)
                pool.affine_select(out=lower[:, :], in_=lower[:, :], compare_op=ALU.is_ge, fill=1.0,
                                   base=0, pattern=[[-1, P]], channel_multiplier=1).then_inc(s["consts_made"], 1)
                pool.affine_select(out=ident[:, :], in_=ident[:, :], compare_op=ALU.not_equal, fill=1.0,
                                   base=0, pattern=[[-1, P]], channel_multiplier=1).then_inc(s["consts_made"], 1)
                pool.iota(gidx[:, :], pattern=[[1, NG]], base=0, channel_multiplier=0,
                          allow_small_or_imprecise_dtypes=True).then_inc(s["consts_made"], 1)
                pool.wait_ge(s["consts_made"], 7)
                pool.memset(Wm[:, :, :], 0.0).then_inc(s["weights_zeroed"], 1)
                pool.memset(L1[:, :], 0.0).then_inc(s["weights_zeroed"], 1)
                pool.memset(G[:, ZB:NB, :, :], 0.0).then_inc(s["G_zeroed"], 1)
                pool.wait_ge(s["zero_sent"], 16)

                def step(t, slot):
                    pool.wait_ge(s[f"staged{slot}"], 4 * (t // 2 + 1))
                    for j in range(SC):
                        pool.indirect_dma_start(rec_dram, bass.IndirectOffsetOnAxis(ap=stage_row[:, slot, j:j + 1], axis=0),
                                                stage[:, slot, j, :], None).then_inc(s[f"scattered{slot}"], 16)

                with pool.Fori(0, NSC // 2) as i:
                    for slot in range(2):
                        pool.wait_ge(s[f"staged{slot}"], 4 * i + 4)
                        pool.sem_inc(s["scatters_begun"], 1)
                        for j in range(SC):
                            pool.indirect_dma_start(
                                rec_dram, bass.IndirectOffsetOnAxis(ap=stage_row[:, slot, j:j + 1], axis=0),
                                stage[:, slot, j, :], None).then_inc(s[f"scattered{slot}"], 16)
                for t in range(NSC // 2 * 2, NSC):
                    step(t, t % 2)
                pool.wait_ge(s["scattered0"], 16 * SC * ((NSC + 1) // 2))
                pool.wait_ge(s["scattered1"], 16 * SC * (NSC // 2))

            @block.tensor
            def _(pe):
                pe.wait_ge(s["consts_made"], 7)
                pe.wait_ge(s["counts_ready"], 1)
                pe.matmul(cps[:, 0, :], lower[:, :], cnt[:, :], start=True, stop=True)
                pe.matmul(cps[:, 1, :], ones[:, :], cnt[:, :], start=True, stop=True).then_inc(s["prefix_ready"], 1)

            @block.scalar
            def _(act):
                act.wait_ge(s["attrs_loaded"], 32)
                act.wait_ge(s["edges_loaded"], 64)
                act.wait_ge(s["rows_ready"], 1)

                def step(c0, slot, value):
                    act.wait_ge(s[f"scattered{slot}"], value) if value is not None else None
                    cols = bass.ds(c0, SC)
                    act.activation(stage_row[:, slot, :], row_f[:, cols], ACT.Copy).then_inc(s[f"staged{slot}"], 1)
                    act.activation(stage[:, slot, :, 0], local[:, cols], ACT.Copy).then_inc(s[f"staged{slot}"], 1)
                    act.activation(stage[:, slot, :, 1].bitcast(i32), dst_i[:, cols], ACT.Copy
                                   ).then_inc(s[f"staged{slot}"], 1)
                    act.activation(stage[:, slot, :, 2:6], ea[:, cols, :], ACT.Copy).then_inc(s[f"staged{slot}"], 1)

                step(0, 0, None)
                step(SC, 1, None)
                act.wait_ge(s["var_ready"], 1)
                act.activation(mv[:, 3, :], mv[:, 1, :], ACT.Sqrt).then_inc(s["std_ready"], 1)
                act.wait_ge(s["weights_loaded"], 16 * n_weights[0])
                ws = s["weights_scaled"]

                def scaled(ap, c):
                    act.activation(ap, ap, ACT.Copy, scale=float(c)).then_inc(ws, 1)

                def scaled_rows(r0, n, c0, w, c):
                    done = 0
                    while done < n:
                        q, p = divmod(r0 + done, P)
                        m = min(n - done, P - p, P if p == 0 else 2 * M1 if p == 2 * M1 else M1)
                        scaled(Wm[p:p + m, q, c0:c0 + w], c)
                        done += m
                scaled_rows(GH, M0, 0, M0, 1 / np.sqrt(M0))
                scaled_rows(GD, M0, 0, M0, 1 / np.sqrt(FAN_M))
                scaled_rows(GV, M1, 0, M0, C3 / np.sqrt(FAN_M))
                for k in range(3):
                    scaled_rows(GH + M0 + k * M1, M1, M0 + k * M1, M1, 1 / np.sqrt(M1))
                    scaled_rows(GD + M0 + k * M1, M1, M0 + k * M1, M1, 1 / np.sqrt(FAN_M))
                    scaled_rows(GR + k * M0, M0, M0 + k * M1, M1, 1 / np.sqrt(FAN_M))
                scaled(W0[:, 0:C0, :], 1 / np.sqrt(FAN0))
                scaled(W0[:, C0:NC, :], C3 / np.sqrt(FAN0))
                scaled(W011[:, :, :], 1 / np.sqrt(FAN1))
                scaled(W101[:, :, :], 1 / np.sqrt(FAN1))
                scaled(L0[:, :], 1 / np.sqrt(M0))
                scaled(L1[:, :], 1 / np.sqrt(M1))
                with act.Fori(1, NSC // 2) as i:
                    for slot in range(2):
                        step(i * (2 * SC) + slot * SC, slot, i * (16 * SC))
                for t in range(NSC // 2 * 2, NSC):
                    step(t * SC, t % 2, 16 * SC * (t // 2))

            @block.vector
            def _(dve):
                n = [0]

                def link(ins):
                    n[0] += 1
                    ins.then_inc(s["v"], 1)
                    dve.wait_ge(s["v"], n[0])

                dve.wait_ge(s["edges_loaded"], 64)
                link(dve.tensor_copy(src_f[:, :], src_i[:, :]))
                link(dve.tensor_scalar(t1[:, :], src_f[:, :], 1.0 / B, 0.5 / B - 0.5, ALU.mult, ALU.add))
                link(dve.tensor_scalar(t2[:, :], t1[:, :], MAGIC, None, ALU.add))
                link(dve.tensor_scalar(blk[:, :], t2[:, :], -MAGIC, None, ALU.add))
                for b in range(NB + 1):
                    ins = dve.tensor_scalar(big[:, b, :], blk[:, :], float(b), 0.0, ALU.is_equal, ALU.add,
                                            accum_out=cnt[:, b:b + 1])
                    n[0] += 1
                    ins.then_inc(s["v"], 1)
                dve.wait_ge(s["v"], n[0])
                dve.sem_inc(s["counts_ready"], 1)
                link(dve.tensor_scalar(t1[:, :], blk[:, :], -float(B), 1.0, ALU.mult, ALU.add))
                link(dve.tensor_tensor(local[:, :], src_f[:, :], t1[:, :], ALU.add))
                dve.wait_ge(s["prefix_ready"], 1)
                ceil0, ceil1, ngr, incl, first, base = (small[:, i, :] for i in range(6))
                link(dve.tensor_scalar(ceil0, cps[:, 1, :], 1.0 / GE, 0.5 - 0.5 / GE, ALU.mult, ALU.add))
                link(dve.tensor_scalar(ceil1, ceil0, MAGIC, None, ALU.add))
                link(dve.tensor_scalar(ngr, ceil1, -MAGIC, None, ALU.add))
                link(dve.memset(small[:, 6, :], 0.0))
                link(dve.tensor_tensor_scan(incl, ngr, small[:, 6, :], 0.0, ALU.add, ALU.add))
                link(dve.tensor_tensor(first, incl, ngr, ALU.subtract))
                link(dve.memset(first[:, NB:NB + 1], float(NG)))
                link(dve.scalar_tensor_tensor(base, first, float(GE), cps[:, 0, :], ALU.mult, ALU.add))
                for b0 in range(0, NB + 1, HB):
                    for b in range(b0, b0 + HB):
                        ins = dve.tensor_tensor_scan(scan[:, b - b0, :], big[:, b, :], big[:, b, :], base[:, b:b + 1],
                                                     ALU.add, ALU.bypass)
                        n[0] += 1
                        ins.then_inc(s["v"], 1)
                    dve.wait_ge(s["v"], n[0])
                    link(dve.tensor_tensor(big[:, b0:b0 + HB, :], big[:, b0:b0 + HB, :], scan[:, :, :], ALU.mult))
                link(dve.tensor_reduce(t2[:, :], big[:, :, :].rearrange("p b t -> p t b"), AX.X, ALU.add))
                link(dve.tensor_scalar(src_f[:, :], t2[:, :], -1.0, None, ALU.add))
                link(dve.tensor_scalar(t1[:, :], src_f[:, :], 1.0 / P, 0.5 / P - 0.5, ALU.mult, ALU.add))
                link(dve.tensor_scalar(t2[:, :], t1[:, :], MAGIC, None, ALU.add))
                link(dve.tensor_scalar(t1[:, :], t2[:, :], -MAGIC, None, ALU.add))
                link(dve.scalar_tensor_tensor(t2[:, :], t1[:, :], -float(P), src_f[:, :], ALU.mult, ALU.add))
                link(dve.scalar_tensor_tensor(row_f[:, :], t2[:, :], float(NT), t1[:, :], ALU.mult, ALU.add))
                link(dve.tensor_scalar(t1[:, :], blk[:, :], float(NB), None, ALU.is_equal))
                link(dve.tensor_scalar(t2[:, :], src_f[:, :], float(DUMP - NG * GE), None, ALU.add))
                link(dve.tensor_tensor(t2[:, :], t2[:, :], row_f[:, :], ALU.subtract))
                link(dve.tensor_tensor(t2[:, :], t2[:, :], t1[:, :], ALU.mult))
                link(dve.tensor_tensor(row_f[:, :], row_f[:, :], t2[:, :], ALU.add))
                dve.sem_inc(s["rows_ready"], 1)
                gview = big[:, :, :].rearrange("p b t -> p (b t)")[:, 0:NB * NG].rearrange("p (b g) -> p g b", b=NB)
                dve.wait_ge(s["consts_made"], 7)
                link(dve.tensor_tensor(gview, gidx[:, :].unsqueeze(2).broadcast_to([P, NG, NB]),
                                       incl[:, None, 0:NB].broadcast_to([P, NG, NB]), ALU.is_ge))
                link(dve.tensor_reduce(gidx[:, :], gview, AX.X, ALU.add))
                link(dve.tensor_scalar(gblk_i[:, :], gidx[:, :], float(NB - 1), None, ALU.min))
                dve.wait_ge(s["nodes_loaded"], 16)
                xv = hx_sb[:, :, :]
                xc = big[0:B, :, :].rearrange("p b t -> p (b t)")[:, 0:NB * D].rearrange("p (b f) -> p b f", f=D)
                sq = scan[0:B, :, :].rearrange("p b t -> p (b t)")[:, 0:NB * D].rearrange("p (b f) -> p b f", f=D)

                def each(a):
                    return a.unsqueeze(2).broadcast_to([B, NB, D])
                link(dve.tensor_reduce(mv[:, 0, :], xv, AX.X, ALU.add))
                link(dve.tensor_scalar(mv[:, 0, :], mv[:, 0, :], 1.0 / D, None, ALU.mult))
                link(dve.tensor_tensor(xc, xv, each(mv[:, 0, :]), ALU.subtract))
                link(dve.tensor_tensor(sq, xc, xc, ALU.mult))
                link(dve.tensor_reduce(mv[:, 1, :], sq, AX.X, ALU.add))
                link(dve.tensor_scalar(mv[:, 1, :], mv[:, 1, :], 1.0 / D, 1e-5, ALU.mult, ALU.add))
                dve.sem_inc(s["var_ready"], 1)
                dve.wait_ge(s["std_ready"], 1)
                link(dve.reciprocal(mv[:, 2, :], mv[:, 3, :]))
                link(dve.tensor_tensor(sq, xc, each(mv[:, 2, :]), ALU.mult))
                link(dve.tensor_scalar(xc, sq, 0.0, None, ALU.max))
                dve.tensor_copy(h_sb[:, :, 0:M0], xc[:, :, 0:M0]).then_inc(s["h_ready"], 1)
                dve.tensor_copy(h_sb[:, :, M0:D].rearrange("p b (k u) -> p b u k", k=3),
                                xc[:, :, M0:D].rearrange("p b (u k) -> p b u k", k=3)).then_inc(s["h_ready"], 1)
                link(dve.tensor_tensor(hx_sb[:, :, :], xv, xc, ALU.add))

        sums = ExitStack()
        rec = sums.enter_context(nc.sbuf_tensor("rec", [P, NSLOT, GT, REC], f32))
        Z = sums.enter_context(nc.sbuf_tensor("Z", [P, NSLOT, GT, GW], f32))
        O = sums.enter_context(nc.sbuf_tensor("O", [P, NSLOT, GT, B], f32))
        rv = sums.enter_context(nc.sbuf_tensor("rv", [P, 2, GT, 3, M1], f32))
        nodes = sums.enter_context(nc.sbuf_tensor("node_numbers", [P, B], f32))
        gp = sums.enter_context(nc.psum_tensor("G_part", [P, 2, 2, 512], f32))
        q = {n: sem(n) for n in (
            "numbers_made", "G_added", "products", "edge_products", "G_part_ready",
            "rv_step", "gathers_begun")}
        rec_in = [sem(f"rec_in{i}") for i in range(NSLOT)]
        gathered = [sem(f"gathered{i}") for i in range(NSLOT)]
        LOOPS, LEFT = divmod(NG, NSLOT)
        assert LEFT and NSLOT % 2 == 0
        rec_rows = rec_dram[0:P * NT, :].rearrange("(p t) c -> p t c", p=P)

        def groups(eng, body):
            with eng.Fori(0, LOOPS) as i:
                for slot in range(NSLOT):
                    body(i * NSLOT + slot, i, slot)
            for slot in range(LEFT):
                body(LOOPS * NSLOT + slot, LOOPS, slot)

        with sums, nc.Block() as block:

            @block.sync
            def _(sp):
                def load(g, turn, slot):
                    sp.wait_ge(q["G_part_ready"], g + 1)
                    sp.dma_start(rec[:, slot, :, :], rec_rows[:, bass.ds(g * GT, GT), :]).then_inc(rec_in[slot], 16)
                groups(sp, load)

            @block.gpsimd
            def _(pool):
                pool.iota(nodes[:, :], pattern=[[1, B]], base=1, channel_multiplier=0,
                          allow_small_or_imprecise_dtypes=True).then_inc(q["numbers_made"], 1)

                def gather(g, turn, slot):
                    pool.wait_ge(q["G_part_ready"], g + 1)
                    pool.wait_ge(rec_in[slot], turn * 16 + 16)
                    pool.sem_inc(q["gathers_begun"], 1)
                    for j in range(GT):
                        pool.indirect_dma_start(
                            Z[:, slot, j, 0:D], None, h_dram,
                            bass.IndirectOffsetOnAxis(ap=rec[:, slot, j, 1:2].bitcast(i32), axis=0)
                        ).then_inc(gathered[slot], 16)
                groups(pool, gather)

            @block.scalar
            def _(act):
                def scale_rows(g, turn, slot):
                    act.wait_ge(gathered[slot], turn * (16 * GT) + 16 * GT)
                    for j in range(GT):
                        act.activation(Z[:, slot, j, GD:GD + D], Z[:, slot, j, GH:GH + D], ACT.Copy,
                                       scale=rec[:, slot, j, 5:6]).then_inc(q["edge_products"], 1)
                        for k in range(1, 3):
                            lo = GR + k * M0
                            act.activation(Z[:, slot, j, lo:lo + M0], Z[:, slot, j, GH:GH + M0], ACT.Copy,
                                           scale=rec[:, slot, j, 2 + k:3 + k]).then_inc(q["edge_products"], 1)
                groups(act, scale_rows)

            @block.tensor
            def _(pe):
                pe.sem_inc(q["G_part_ready"], NSLOT)

                def product(g, turn, slot):
                    pe.wait_ge(q["products"], 3 * g + 3)
                    pe.wait_ge(q["edge_products"], 3 * GT * g + 3 * GT)
                    pe.wait_ge(q["G_added"], g + 1)
                    for j in range(GT):
                        for i in range(2):
                            last = pe.matmul(gp[0:B, slot % 2, i, 0:HALF], O[:, slot, j, :],
                                             Z[:, slot, j, i * HALF:(i + 1) * HALF], start=j == 0, stop=j == GT - 1)
                    last.then_inc(q["G_part_ready"], 1)
                groups(pe, product)

            @block.vector
            def _(dve):
                dve.sem_inc(q["G_added"], 2)
                dve.wait_ge(q["numbers_made"], 1)

                def add(g, slot, at):
                    dve.wait_ge(q["G_part_ready"], g + 1 + NSLOT)
                    dve.wait_ge(q["G_added"], g + 2)
                    dve.tensor_tensor(G[0:B, bass.ds(at, 1), :, :], G[0:B, bass.ds(at, 1), :, :],
                                      gp[0:B, slot % 2:slot % 2 + 1, :, 0:HALF], ALU.add).then_inc(q["G_added"], 1)

                def products(g, turn, slot):
                    c = rec[:, slot, :, :]
                    zs = Z[:, slot, :, :]
                    h = slot % 2
                    dve.wait_ge(rec_in[slot], turn * 16 + 16)
                    dve.wait_ge(q["G_part_ready"], g + 1)
                    dve.tensor_tensor(O[:, slot, :, :], nodes[:, None, :].broadcast_to([P, GT, B]),
                                      c[:, :, 0:1].broadcast_to([P, GT, B]), ALU.is_equal).then_inc(q["products"], 1)
                    dve.wait_ge(gathered[slot], turn * (16 * GT) + 16 * GT)
                    dve.tensor_tensor(rv[:, h, :, :, :], zs[:, :, M0:D].rearrange("p j (k u) -> p j k u", k=3),
                                      c[:, :, 2:5].unsqueeze(3).broadcast_to([P, GT, 3, M1]), ALU.mult
                                      ).then_inc(q["rv_step"], 1)
                    dve.tensor_tensor(zs[:, :, GR:GR + M0], zs[:, :, 0:M0], c[:, :, 2:3].broadcast_to([P, GT, M0]),
                                      ALU.mult).then_inc(q["products"], 1)
                    dve.wait_ge(q["rv_step"], g + 1)
                    dve.tensor_reduce(zs[:, :, GV:GW], rv[:, h, :, :, :].rearrange("p j k u -> p j u k"), AX.X, ALU.add
                                      ).then_inc(q["products"], 1)

                def block_numbers(g0, n):
                    return nc.values_load_multi_w_load_instructions(
                        gblk_i[0:1, bass.ds(g0, n)], engines=[mybir.EngineType.DVE], min_val=0, max_val=NB - 1)[1]

                products(0, 0, 0)
                with dve.Fori(0, LOOPS) as i:
                    at = block_numbers(i * NSLOT, NSLOT)
                    for slot in range(NSLOT):
                        g = i * NSLOT + slot
                        products(g + 1, i + (slot + 1) // NSLOT, (slot + 1) % NSLOT)
                        add(g, slot, at[slot])
                at = block_numbers(LOOPS * NSLOT, LEFT)
                for slot in range(LEFT):
                    if slot < LEFT - 1:
                        products(LOOPS * NSLOT + slot + 1, LOOPS, slot + 1)
                    add(LOOPS * NSLOT + slot, slot, at[slot])

        up = ExitStack()

        def ub(name, shape):
            return up.enter_context(nc.sbuf_tensor(name, shape, f32))
        Gs = ub("Gs", [B, 2, GW])
        hs = ub("hs", [B, 2, D])
        GT_ = ub("GT", [P, 2, NCH, B])
        h0T = ub("h0T", [M0, 2, B])
        h1T = ub("h1T", [V, 2, B])
        a_sb = ub("agg", [B, 2, D])
        a0T = ub("a0T", [M0, 2, B])
        C = ub("C", [B, 2, 3, 2 * M1])
        pairs = ub("pairs", [B, 2, NC * P])
        q3 = ub("q3", [B, 3, M1 * M1])
        PT = ub("PT", [P, 2, TQ, B])
        prod = ub("prod", [B, 3, 2 * M1, M1])
        vsum = ub("vsum", [B, 2, 3, M1])
        o1 = ub("o1", [B, 2, V])
        sums_sb = ub("sums_sb", [B, 2, D])
        res = ub("res", [B, 2, D])
        psA = up.enter_context(nc.psum_tensor("psA", [P, 512], f32))
        psO = up.enter_context(nc.psum_tensor("psO", [P, 512], f32))
        psT = up.enter_context(nc.psum_tensor("psT", [P, 4, 512], f32))
        psP = up.enter_context(nc.psum_tensor("psP", [P, 2, 512], f32))
        u = {n: sem(n) for n in (
            "block_staged", "preparing", "prepared", "T_ready", "products_made", "vsum_ready",
            "pairs_by_vector", "pairs_by_pool", "pairs_by_scalar", "pool_step", 
            "chunks_transposed", "chunks_copied", "chunks_summed", "o1_ready", "res_ready", "res_stored",
            "a0_transposes_begun", "sums_copied")}
        NPREP = 8
        out_v = out.rearrange("(b p) f -> p b f", p=B)

        PREP_AT = (0, 1, 2, 3)
        T_AT = 4
        stored = [sem("stored0"), sem("stored1")]

        def pipelined(eng, step):
            loops = (NB - 2) // 2
            with eng.Fori(0, loops) as i:
                for slot in range(2):
                    step(i * 2 + slot, slot, i * 2 + slot + 1)
            for b in range(2 * loops, NB):
                step(b, b % 2, b + 1 if b + 1 < NB else None)

        def pairs_free(b):
            return 1 if isinstance(b, int) and b == 0 else b * NQ - NQ + 2

        with up, nc.Block() as block:

            @block.scalar
            def _(act):
                act.sem_inc(u["chunks_copied"], 2)
                act.sem_inc(u["prepared"], 1)
                act.sem_inc(u["sums_copied"], 1)

                def stage(b, slot):
                    act.activation(Gs[:, slot, :], G[0:B, bass.ds(b, 1), :, :].rearrange("p b i f -> p (b i f)"),
                                   ACT.Copy).then_inc(u["block_staged"], 1)
                    act.activation(hs[:, slot, :], h_sb[:, bass.ds(b, 1), :].rearrange("p b f -> p (b f)"),
                                   ACT.Copy).then_inc(u["block_staged"], 1)

                def prepare(b, slot, part):
                    act.wait_ge(u["preparing"], 4 * b + 1 + part)

                    def copy(dst, of):
                        act.activation(dst, of, ACT.Copy).then_inc(u["prepared"], 1)
                    if part == 0:
                        copy(GT_[:, slot, 0:4, :], psA[:, 0:4 * B].rearrange("p (c n) -> p c n", c=4))
                    elif part == 1:
                        copy(GT_[0:GREST, slot, 4, :], psA[0:GREST, 0:B])
                        copy(h0T[:, slot, :], psA[0:M0, B:2 * B])
                        copy(h1T[:, slot, :], psA[0:V, 2 * B:3 * B])
                    elif part == 2:
                        copy(a_sb[:, slot, :], psA[0:B, 0:D])
                        copy(C[:, slot, :, 0:M1], psA[0:B, M0:D].rearrange("p (k u) -> p k u", k=3))
                        copy(C[:, slot, :, M1:2 * M1], hs[:, slot, M0:D].rearrange("p (k u) -> p k u", k=3))
                    else:
                        copy(a0T[:, slot, :], psA[0:M0, 0:B])

                def pair(b, slot, r):
                    row = M0 - VP - VA + r
                    act.activation(pairs[:, slot, row * M0:(row + 1) * M0], a_sb[:, slot, 0:M0], ACT.Copy,
                                   scale=hs[:, slot, row:row + 1]).then_inc(u["pairs_by_scalar"], 1)

                def all_pairs(b, slot, rows):
                    act.wait_ge(u["prepared"], NPREP * b + 8)
                    for r in rows:
                        pair(b, slot, r)

                def step(b, slot, nxt):
                    for c in range(NQ):
                        act.wait_ge(u["chunks_transposed"], b * NQ + c + 1)
                        act.wait_ge(u["chunks_summed"], b * NQ + c + 1)
                        act.activation(PT[:, c % 2, :, :], psP[:, c % 2, 0:TQ * B].rearrange("p (c n) -> p c n", c=TQ),
                                       ACT.Copy).then_inc(u["chunks_copied"], 1)
                        if nxt is not None:
                            if c in PREP_AT:
                                prepare(nxt, 1 - slot, PREP_AT.index(c))
                            if c >= NQ - VA // 3:
                                r = 3 * (c - NQ + VA // 3)
                                all_pairs(nxt, 1 - slot, range(r, r + 3))
                    act.wait_ge(u["chunks_summed"], b * NQ + NQ + 2)
                    act.activation(sums_sb[:, slot, :], psO[0:B, 0:D], ACT.Copy).then_inc(u["sums_copied"], 1)
                    if not isinstance(b, int) or b + 2 < NB:
                        stage(b + 2, slot)

                stage(0, 0)
                for part in range(4):
                    prepare(0, 0, part)
                all_pairs(0, 0, range(VA))
                stage(1, 1)
                pipelined(act, step)

            @block.tensor
            def _(pe):
                pe.sem_inc(u["chunks_summed"], 2)
                idn = ident[0:B, 0:B]

                def prepare(b, slot, part):
                    if part == 0:
                        pe.wait_ge(u["block_staged"], 2 * b + 2)
                        pe.wait_ge(u["prepared"], NPREP * b + 1)
                        for c in range(4):
                            last = pe.transpose(psA[:, c * B:(c + 1) * B], Gs[:, slot, c * P:(c + 1) * P], idn)
                    elif part == 1:
                        pe.wait_ge(u["prepared"], NPREP * b + 2)
                        pe.transpose(psA[0:GREST, 0:B], Gs[:, slot, 4 * P:GW], idn)
                        pe.transpose(psA[0:M0, B:2 * B], hs[:, slot, 0:M0], idn)
                        last = pe.transpose(psA[0:V, 2 * B:3 * B], hs[:, slot, M0:D], idn)
                    elif part == 2:
                        pe.wait_ge(u["prepared"], NPREP * b + 5)
                        for c in range(NCH):
                            k = P if c < NCH - 1 else GREST
                            last = pe.matmul(psA[0:B, 0:D], GT_[0:k, slot, c, :], Wm[0:k, c, :],
                                             start=c == 0, stop=c == NCH - 1)
                    else:
                        pe.wait_ge(u["prepared"], NPREP * b + 8)
                        pe.sem_inc(u["a0_transposes_begun"], 1)
                        last = pe.transpose(psA[0:M0, 0:B], a_sb[:, slot, 0:M0], idn)
                    last.then_inc(u["preparing"], 1)

                def first_products(b, slot):
                    pe.wait_ge(u["products_made"], 3 * b + 1)
                    pe.wait_ge(u["prepared"], NPREP * b + 9)
                    for i in range(2):
                        pe.matmul(psT[0:B, i, :], h0T[:, slot, :],
                                  W011[:, i * 16:(i + 1) * 16, :].rearrange("p v w -> p (v w)"), start=True, stop=True)
                    for i in range(2):
                        last = pe.matmul(psT[0:B, 2 + i, :], a0T[:, slot, :],
                                         W101[:, i * 16:(i + 1) * 16, :].rearrange("p u w -> p (u w)"),
                                         start=True, stop=True)
                    last.then_inc(u["T_ready"], 1)

                def linear(b, slot):
                    pe.wait_ge(u["sums_copied"], b + 1)
                    pe.matmul(psO[0:B, M0:D], h1T[:, slot, :], L1[:, :], start=True, stop=True)
                    pe.matmul(psO[0:B, 0:M0], h0T[:, slot, :], L0[:, :], start=True, stop=False)

                def step(b, slot, nxt):
                    pe.wait_ge(u["pairs_by_vector"], b + 1)
                    pe.wait_ge(u["pairs_by_scalar"], VA * b + VA)
                    pe.wait_ge(u["pairs_by_pool"], 2 * b + 3)
                    for c in range(NQ + 1):
                        if c < NQ:
                            pe.wait_ge(u["chunks_copied"], b * NQ + c + 1)
                            for m in range(TQ):
                                ch = c * TQ + m
                                last = pe.transpose(psP[:, c % 2, m * B:(m + 1) * B],
                                                    pairs[:, slot, ch * P:(ch + 1) * P], idn)
                            last.then_inc(u["chunks_transposed"], 1)
                        if nxt is not None and c in PREP_AT:
                            prepare(nxt, 1 - slot, PREP_AT.index(c))
                        if nxt is not None and c == T_AT:
                            first_products(nxt, 1 - slot)
                        if c == 1:
                            linear(b, slot)
                        if c > 0:
                            pe.wait_ge(u["chunks_copied"], b * NQ + c + 2)
                            for m in range(TQ):
                                ch = (c - 1) * TQ + m
                                last = pe.matmul(psO[0:B, 0:M0], PT[:, (c - 1) % 2, m, :], W0[:, ch, :],
                                                 start=False, stop=ch == NC - 1)
                            last.then_inc(u["chunks_summed"], 1)

                for part in range(4):
                    prepare(0, 0, part)
                first_products(0, 0)
                pipelined(pe, step)

            @block.gpsimd
            def _(pool):
                pool.sem_inc(u["pairs_by_pool"], 1)

                def make_pairs(b, slot):
                    pool.wait_ge(u["prepared"], NPREP * b + 8)
                    pool.wait_ge(u["chunks_summed"], pairs_free(b))
                    pool.wait_ge(u["pairs_by_pool"], 2 * b + 1)
                    a, h = a_sb[:, slot, :], hs[:, slot, :]
                    for k in range(3):
                        lo = M0 + k * M1
                        pool.tensor_tensor(q3[:, k, :].rearrange("p (u v) -> p u v", v=M1),
                                           h[:, lo:lo + M1].unsqueeze(2).broadcast_to([B, M1, M1]),
                                           a[:, None, lo:lo + M1].broadcast_to([B, M1, M1]), ALU.mult
                                           ).then_inc(u["pool_step"], 1)
                    pool.wait_ge(u["pool_step"], 4 * b + 3)
                    pool.tensor_tensor(q3[:, 0, :], q3[:, 0, :], q3[:, 1, :], ALU.add).then_inc(u["pool_step"], 1)
                    pool.wait_ge(u["pool_step"], 4 * b + 4)
                    pool.tensor_tensor(pairs[:, slot, C0 * P:NC * P], q3[:, 0, :], q3[:, 2, :], ALU.add
                                       ).then_inc(u["pairs_by_pool"], 1)
                    pool.tensor_tensor(pairs[:, slot, (M0 - VP) * M0:M0 * M0].rearrange("p (u v) -> p u v", v=M0),
                                       h[:, M0 - VP:M0].unsqueeze(2).broadcast_to([B, VP, M0]),
                                       a[:, None, 0:M0].broadcast_to([B, VP, M0]), ALU.mult
                                       ).then_inc(u["pairs_by_pool"], 1)

                def step(b, slot, nxt):
                    if nxt is not None:
                        make_pairs(nxt, 1 - slot)
                make_pairs(0, 0)
                pipelined(pool, step)

            @block.vector
            def _(dve):
                dve.sem_inc(u["products_made"], 1)
                dve.sem_inc(u["res_ready"], 3)
                dve.sem_inc(u["vsum_ready"], 1)

                def make_pairs(b, slot):
                    dve.wait_ge(u["prepared"], NPREP * b + 8)
                    dve.wait_ge(u["chunks_summed"], pairs_free(b))
                    rows = M0 - VP - VA
                    dve.tensor_tensor(pairs[:, slot, 0:rows * M0].rearrange("p (u v) -> p u v", v=M0),
                                      hs[:, slot, 0:rows].unsqueeze(2).broadcast_to([B, rows, M0]),
                                      a_sb[:, slot, None, 0:M0].broadcast_to([B, rows, M0]), ALU.mult
                                      ).then_inc(u["pairs_by_vector"], 1)

                def second_products(b, slot):
                    dve.wait_ge(u["T_ready"], b + 1)
                    dve.wait_ge(u["vsum_ready"], b + 1)
                    for k in range(3):
                        dve.tensor_tensor(
                            prod[:, k, :, :], psT[0:B, :, :].rearrange("p i (c w) -> p (i c) w", w=M1),
                            C[:, slot, k, :].unsqueeze(2).broadcast_to([B, 2 * M1, M1]), ALU.mult
                        ).then_inc(u["products_made"], 1)

                def vector_sums(b, slot):
                    dve.wait_ge(u["products_made"], 3 * b + 4)
                    dve.tensor_reduce(vsum[:, slot, :, :], prod[:, :, :, :].rearrange("p k c w -> p k w c"), AX.X, ALU.add
                                      ).then_inc(u["vsum_ready"], 1)

                def finish(b, slot):
                    at = bass.ds(b, 1)
                    o, ps = res[:, slot, :], sums_sb[:, slot, :]
                    dve.wait_ge(u["sums_copied"], b + 2)
                    dve.wait_ge(u["res_stored"], b + 1)
                    dve.wait_ge(u["vsum_ready"], b + 2)
                    dve.tensor_tensor(o1[:, slot, :], ps[:, M0:D], vsum[:, slot, :, :].rearrange("p k w -> p (k w)"),
                                      ALU.add).then_inc(u["o1_ready"], 1)
                    dve.tensor_tensor(o[:, None, 0:M0], ps[:, None, 0:M0], hx_sb[:, at, 0:M0], ALU.add
                                      ).then_inc(u["res_ready"], 1)
                    dve.wait_ge(u["o1_ready"], b + 1)
                    dve.tensor_tensor(o[:, None, M0:D].rearrange("p b (u k) -> p b u k", k=3),
                                      o1[:, slot, None, :].rearrange("p b (k u) -> p b u k", k=3),
                                      hx_sb[:, at, M0:D].rearrange("p b (u k) -> p b u k", k=3), ALU.add
                                      ).then_inc(u["res_ready"], 1)

                def step(b, slot):
                    second_products(b, slot)
                    if not isinstance(b, int) or b > 0:
                        finish(b - 1, 1 - slot)
                    vector_sums(b, slot)
                    if not isinstance(b, int) or b + 1 < NB:
                        make_pairs(b + 1, 1 - slot)

                make_pairs(0, 0)
                step(0, 0)
                loops = (NB - 2) // 2
                with dve.Fori(0, loops) as i:
                    for n in range(2):
                        step(i * 2 + n + 1, 1 - n)
                for b in range(2 * loops + 1, NB):
                    step(b, b % 2)
                finish(NB - 1, (NB - 1) % 2)

            @block.sync
            def _(sp):
                sp.sem_inc(u["res_stored"], 2)

                def store(b, slot, nxt):
                    sp.wait_ge(u["res_ready"], 2 * b + 5)
                    sp.dma_start(out_v[:, bass.ds(b, 1), :], res[:, slot, None, :]).then_inc(stored[slot], 16)
                    sp.wait_ge(stored[slot], (b - slot) * 8 + 16)
                    sp.sem_inc(u["res_stored"], 1)
                pipelined(sp, store)
                sp.wait_ge(stored[0], 16 * ((NB + 1) // 2))
                sp.wait_ge(stored[1], 16 * (NB // 2))


_INS = ["x", "src", "dst", "edge_attr_4"] + ["L0_gnn_" + n for n in (
    "wm000", "wm011", "wm101", "wm110", "lm0", "lm1", "wu000", "wu011", "wu101", "wu110", "lu0", "lu1")]


def kernel(**inputs):
    import concourse.bacc as _bacc
    from concourse.bass_utils import run_bass_kernel_spmd as _run

    nc = _bacc.Bacc("TRN2", target_bir_lowering=False, num_devices=1)
    arrays, args = {}, []
    for name in _INS:
        a = np.ascontiguousarray(inputs[name])
        arrays[f"in_{name}"] = a
        args.append(nc.dram_tensor(f"in_{name}", a.shape, mybir.dt.from_np(a.dtype), kind="ExternalInput").ap())
    shape = arrays["in_x"].shape
    args.append(nc.dram_tensor("out", shape, mybir.dt.float32, kind="ExternalOutput").ap())
    gnn_layer(nc, *args)
    r = _run(nc, [arrays], core_ids=[0])
    return r.results[0]["out"]
```

```python
from contextlib import ExitStack

import numpy as np

import concourse.bass as bass
from concourse import mybir


def gnn_layer(nc, x, src, dst, edge_attr, wm000, wm011, wm101, wm110, lm0, lm1,
              wu000, wu011, wu101, wu110, lu0, lu1, out):
    f32, i32 = mybir.dt.float32, mybir.dt.int32
    ALU, ACT, AX = mybir.AluOpType, mybir.ActivationFunctionType, mybir.AxisListType

    N, D = x.shape
    E = src.shape[0]
    M0, M1 = lm0.shape[0], lm1.shape[0]
    V = 3 * M1
    P = 128
    NB = 25
    B = N // NB
    assert B * NB == N and B <= P and M0 + V == D

    EC = -(-E // P)
    TAIL = E - (P - 1) * EC
    assert 0 < TAIL <= EC
    SC = 17
    NSC = EC // SC
    assert NSC * SC == EC
    REC = 6
    GT = 2
    GE = GT * P
    NG = (E - NB) // GE + NB
    NSLOT = 8
    NPART = 4
    AHEAD = 3
    NT = NG * GT
    DUMP = P * NT
    NPAD = P * EC - E
    GH, GD, GR, GV = 0, D, 2 * D, 2 * D + 3 * M0
    GW = GV + M1
    HALF = GW // 2
    NCH = -(-GW // P)
    GREST = GW - (NCH - 1) * P
    MAGIC = 12582912.0
    FAN_M = M0 + M1
    FAN0 = M0 * M0 + M1 * M1
    FAN1 = 2 * M0 * M1
    C3 = 1.0 / np.sqrt(3.0)
    C0 = M0 * M0 // P
    C1 = M1 * M1 // P
    NC = C0 + C1
    TQ = 4
    HC = 16
    VA = M0 - 2 * HC
    VF = 16
    NTC = NC - HC
    NQ = NTC // TQ
    assert 2 * M0 == P and NQ * TQ == NTC and VA % (2 * TQ) == 0 and VF % (2 * TQ) == 0

    h_dram = nc.dram_tensor("h_dram", (N, D), f32, kind="Internal").ap()
    t011_dram = nc.dram_tensor("t011_dram", (NB, B, M1 * M1), f32, kind="Internal").ap()
    h0t_dram = nc.dram_tensor("h0t_dram", (NB, M0, B), f32, kind="Internal").ap()
    rec_dram = nc.dram_tensor("rec_dram", (P * NT + NPAD, REC), f32, kind="Internal").ap()

    ctx = ExitStack()
    with ctx:
        def sb(name, shape, dt=f32):
            return ctx.enter_context(nc.sbuf_tensor(name, shape, dt))

        def sem(name):
            return ctx.enter_context(nc.semaphore(name))

        hx_sb = sb("hx_sb", [B, NB, D])
        G = sb("G", [P, NB, 2, HALF])
        ident = sb("ident", [P, P])
        Wm = sb("Wm", [P, NCH, D])
        W0 = sb("W0", [P, NC, M0])
        W101 = sb("W101", [M0, M1, M1])
        gblk_i = sb("gblk_i", [P, NG], i32)

        s = {n: sem(n) for n in (
            "nodes_loaded", "edges_loaded", "attrs_loaded", "zero_sent", "weights_loaded", "edge_memset",
            "consts_made", "weights_zeroed", "weights_scaled", "v", "counts_ready", "prefix_ready",
            "blocks_ready", "local_begun", "rows_ready", "h_ready", "h_stored", "var_ready", "std_ready",
            "scatters_begun", "staged0", "staged1", "scattered0", "scattered1", "G_zeroed")}
        hp = {n: sem(n) for n in (
            "h_staged", "h_transposed", "h_copied", "T011_ready", "T011_staged", "T011_stored",
            "linear_ready", "linear_added", "h0T_stored")}

        n_weights, loads, n_scaled = [], [], []
        EARLY = SC
        NEXT = 4 * SC
        HB = (NB + 1) // 2
        assert (NB + 1) * (NEXT - EARLY) <= HB * EC
        ZB = -(-NT * REC // GW)
        early = ExitStack()

        def eb(name, shape, dt=f32):
            return early.enter_context(nc.sbuf_tensor(name, shape, dt))
        h_sb = eb("h_sb", [B, NB, D])
        src_i = eb("src_i", [P, EC], i32)
        dst_i = eb("dst_i", [P, EC], i32)
        ea = eb("ea", [P, EC, 4])
        src_f = eb("src_f", [P, EC])
        blk = eb("blk", [P, EC])
        t1 = eb("t1", [P, EC])
        t2 = eb("t2", [P, EC])
        local = eb("local", [P, EC])
        row_f = eb("row_f", [P, EC])
        lower = eb("lower", [P, P])
        ones = eb("ones", [P, P])
        cnt = eb("cnt", [P, NB + 1])
        small = eb("small", [P, 8, NB + 1])
        gidx = eb("gidx", [P, NG])
        stage = eb("stage", [P, 2, SC, REC])
        stage_row = eb("stage_row", [P, 2, SC], i32)
        mv = eb("mv", [B, 4, NB])
        carry = eb("carry", [P, NB + 1])
        hst = eb("h_block", [B, D])
        h0T = eb("h0T", [M0, B])
        h1T = eb("h1T", [V, B])
        W011 = eb("W011", [M0, M1, M1])
        L0 = eb("L0", [M0, M0])
        L1 = eb("L1", [V, V])

        big = early.enter_context(nc.sbuf_tensor("one_hot_blocks", [P, NB + 1, EC], f32))
        scan = early.enter_context(nc.sbuf_tensor("running_places", [P, HB, EC], f32))
        tst = scan[0:B, :, :].rearrange("p b t -> p (b t)")[:, 0:M1 * M1]
        cps_bank = early.enter_context(nc.psum_tensor("count_prefix", [P, 512], f32))
        cps = cps_bank[:, 0:2 * (NB + 1)].rearrange("p (i b) -> p i b", i=2)
        psH = early.enter_context(nc.psum_tensor("psH", [P, 512], f32))
        psL = early.enter_context(nc.psum_tensor("psL", [P, 512], f32))
        psT0 = early.enter_context(nc.psum_tensor("psT0", [P, 2, 512], f32))
        with early, nc.Block() as block:

            @block.sync
            def _(sp):
                sp.wait_ge(s["edge_memset"], 3)
                for tile, dram in ((src_i, src), (dst_i, dst)):
                    sp.dma_start(tile[0:P - 1, :], dram[0:(P - 1) * EC].rearrange("(p t) -> p t", t=EC)
                                 ).then_inc(s["edges_loaded"], 16)
                    sp.dma_start(tile[P - 1:P, 0:TAIL], dram[(P - 1) * EC:E].rearrange("(p t) -> p t", p=1)
                                 ).then_inc(s["edges_loaded"], 16)
                sp.dma_start(ea[0:P - 1, :, :], edge_attr[0:(P - 1) * EC, :].rearrange("(p t) c -> p t c", t=EC)
                             ).then_inc(s["attrs_loaded"], 16)
                sp.dma_start(ea[P - 1:P, 0:TAIL, :], edge_attr[(P - 1) * EC:E, :].rearrange("(p t) c -> p t c", p=1)
                             ).then_inc(s["attrs_loaded"], 16)
                sp.dma_start(hx_sb[:, :, :], x.rearrange("(b p) f -> p b f", p=B)).then_inc(s["nodes_loaded"], 16)
                sp.wait_ge(s["consts_made"], 1)
                sp.dma_start(rec_dram[0:P * NT, :].rearrange("(p t) c -> p (t c)", p=P),
                             G[:, 0:ZB, :, :].rearrange("p b i f -> p (b i f)")[:, 0:NT * REC]
                             ).then_inc(s["zero_sent"], 16)
                sp.wait_ge(s["weights_zeroed"], 2)
                wl = s["weights_loaded"]
                def rows(r0, n, c0, w):
                    done = 0
                    while done < n:
                        c, p = divmod(r0 + done, P)
                        m = min(n - done, P - p)
                        sp.dma_start(Wm[p:p + m, c, c0:c0 + w.shape[1]], w[done:done + m, :]).then_inc(wl, 16)
                        done += m
                        loads.append(1)
                rows(GH, M0, 0, lm0)
                rows(GD, M0, 0, wm000[:, 0, :])
                rows(GV, M1, 0, wm110[:, 0, :])
                for k in range(3):
                    rows(GH + M0 + k * M1, M1, M0 + k * M1, lm1)
                    rows(GD + M0 + k * M1, M1, M0 + k * M1, wm101[:, 0, :])
                    rows(GR + k * M0, M0, M0 + k * M1, wm011[:, 0, :])
                    sp.dma_start(L1[k * M1:(k + 1) * M1, k * M1:(k + 1) * M1], lu1).then_inc(wl, 16)
                sp.dma_start(L0[:, :], lu0).then_inc(wl, 16)
                for i in range(2):
                    sp.dma_start(W0[i * M0:(i + 1) * M0, 0:HC, :],
                                 wu000[i * HC:(i + 1) * HC].rearrange("u v w -> v u w")).then_inc(wl, 16)
                sp.dma_start(W0[:, HC:C0, :],
                             wu000[2 * HC:M0].rearrange("u v w -> (u v) w").rearrange("(c p) w -> p c w", p=P)
                             ).then_inc(wl, 16)
                sp.dma_start(W0[:, C0:NC, :], wu110.rearrange("u v w -> (u v) w").rearrange("(c p) w -> p c w", p=P)
                             ).then_inc(wl, 16)
                sp.dma_start(W011[:, :, :], wu011).then_inc(wl, 16)
                sp.dma_start(W101[:, :, :], wu101.rearrange("u v w -> v u w")).then_inc(wl, 16)
                n_weights.append(len(loads) + 3 + 7)
                sp.wait_ge(s["h_ready"], 2)
                sp.dma_start(h_dram.rearrange("(b p) f -> p b f", p=B), h_sb[:, :, :]).then_inc(s["h_stored"], 16)
                sp.sem_inc(hp["h0T_stored"], 16)
                sp.sem_inc(hp["T011_stored"], 16)
                with sp.Fori(0, NB) as b:
                    sp.wait_ge(hp["h_copied"], 2 * b + 2)
                    sp.dma_start(h0t_dram[bass.ds(b, 1), :, :].rearrange("b p f -> p b f"), h0T[:, None, :]
                                 ).then_inc(hp["h0T_stored"], 16)
                    sp.wait_ge(hp["T011_staged"], b + 2)
                    sp.dma_start(t011_dram[bass.ds(b, 1), :, :].rearrange("b p f -> p b f"), tst[:, None, :]
                                 ).then_inc(hp["T011_stored"], 16)
                sp.wait_ge(s["h_stored"], 16)
                sp.wait_ge(hp["T011_stored"], 16 * NB + 16)
                sp.wait_ge(hp["h0T_stored"], 16 * NB + 16)
            
            @block.gpsimd
            def _(pool):
                pool.memset(src_i[96:P, TAIL:EC], N).then_inc(s["edge_memset"], 1)
                pool.memset(dst_i[96:P, TAIL:EC], 0).then_inc(s["edge_memset"], 1)
                pool.memset(ea[96:P, TAIL:EC, :], 0.0).then_inc(s["edge_memset"], 1)
                pool.wait_ge(s["edge_memset"], 3)
                pool.memset(G[:, 0:ZB, :, :], 0.0).then_inc(s["consts_made"], 1)
                pool.memset(ones[:, :], 1.0).then_inc(s["consts_made"], 1)
                pool.memset(lower[:, :], 0.0).then_inc(s["consts_made"], 1)
                pool.memset(ident[:, :], 0.0).then_inc(s["consts_made"], 1)
                pool.wait_ge(s["consts_made"], 4)
                pool.affine_select(out=lower[:, :], in_=lower[:, :], compare_op=ALU.is_ge, fill=1.0,
                                   base=0, pattern=[[-1, P]], channel_multiplier=1).then_inc(s["consts_made"], 1)
                pool.affine_select(out=ident[:, :], in_=ident[:, :], compare_op=ALU.not_equal, fill=1.0,
                                   base=0, pattern=[[-1, P]], channel_multiplier=1).then_inc(s["consts_made"], 1)
                pool.iota(gidx[:, :], pattern=[[1, NG]], base=0, channel_multiplier=0,
                          allow_small_or_imprecise_dtypes=True).then_inc(s["consts_made"], 1)
                pool.wait_ge(s["consts_made"], 7)
                pool.memset(Wm[:, :, :], 0.0).then_inc(s["weights_zeroed"], 1)
                pool.memset(L1[:, :], 0.0).then_inc(s["weights_zeroed"], 1)
                pool.memset(G[:, ZB:NB, :, :], 0.0).then_inc(s["G_zeroed"], 1)
                pool.wait_ge(s["zero_sent"], 16)

                def step(slot, staged):
                    pool.wait_ge(s[f"staged{slot}"], staged)
                    pool.sem_inc(s["scatters_begun"], 1)
                    for j in range(SC):
                        pool.indirect_dma_start(
                            rec_dram, bass.IndirectOffsetOnAxis(ap=stage_row[:, slot, j:j + 1], axis=0),
                            stage[:, slot, j, :], None).then_inc(s[f"scattered{slot}"], 16)

                with pool.Fori(0, NSC // 2) as i:
                    for slot in range(2):
                        step(slot, 4 * i + 4)
                for t in range(NSC // 2 * 2, NSC):
                    step(t % 2, 4 * (t // 2 + 1))
                pool.wait_ge(s["scattered0"], 16 * SC * ((NSC + 1) // 2))
                pool.wait_ge(s["scattered1"], 16 * SC * (NSC // 2))

            @block.scalar
            def _(act):
                act.wait_ge(s["blocks_ready"], 1)
                act.activation(local[:, :], blk[:, :], ACT.Copy, scale=-float(B), bias=1.0).then_inc(s["local_begun"], 1)
                act.wait_ge(s["attrs_loaded"], 32)
                act.wait_ge(s["edges_loaded"], 64)
                act.wait_ge(s["rows_ready"], 1)

                def step(c0, slot, value):
                    if value is not None:
                        act.wait_ge(s[f"scattered{slot}"], value)
                    cols = bass.ds(c0, SC)
                    act.activation(stage_row[:, slot, :], row_f[:, cols], ACT.Copy).then_inc(s[f"staged{slot}"], 1)
                    act.activation(stage[:, slot, :, 0], local[:, cols], ACT.Copy).then_inc(s[f"staged{slot}"], 1)
                    act.activation(stage[:, slot, :, 1].bitcast(i32), dst_i[:, cols], ACT.Copy
                                   ).then_inc(s[f"staged{slot}"], 1)
                    act.activation(stage[:, slot, :, 2:6], ea[:, cols, :], ACT.Copy).then_inc(s[f"staged{slot}"], 1)

                step(0, 0, None)
                act.wait_ge(s["rows_ready"], 2)
                step(SC, 1, None)
                step(2 * SC, 0, 16 * SC)
                step(3 * SC, 1, 16 * SC)
                act.wait_ge(s["var_ready"], 1)
                act.activation(mv[:, 3, :], mv[:, 1, :], ACT.Sqrt).then_inc(s["std_ready"], 1)
                act.wait_ge(s["weights_loaded"], 16 * n_weights[0])
                ws = s["weights_scaled"]

                n_scaled.append(0)

                def scaled(ap, c):
                    n_scaled[0] += 1
                    act.activation(ap, ap, ACT.Copy, scale=float(c)).then_inc(ws, 1)

                def scaled_rows(r0, n, c0, w, c):
                    done = 0
                    while done < n:
                        q, p = divmod(r0 + done, P)
                        m = min(n - done, P - p, P if p == 0 else 2 * M1 if p == 2 * M1 else M1)
                        scaled(Wm[p:p + m, q, c0:c0 + w], c)
                        done += m
                scaled_rows(GH, M0, 0, M0, 1 / np.sqrt(M0))
                scaled_rows(GD, M0, 0, M0, 1 / np.sqrt(FAN_M))
                scaled_rows(GV, M1, 0, M0, C3 / np.sqrt(FAN_M))
                for k in range(3):
                    scaled_rows(GH + M0 + k * M1, M1, M0 + k * M1, M1, 1 / np.sqrt(M1))
                    scaled_rows(GD + M0 + k * M1, M1, M0 + k * M1, M1, 1 / np.sqrt(FAN_M))
                    scaled_rows(GR + k * M0, M0, M0 + k * M1, M1, 1 / np.sqrt(FAN_M))
                scaled(W0[:, 0:C0, :], 1 / np.sqrt(FAN0))
                scaled(W0[:, C0:NC, :], C3 / np.sqrt(FAN0))
                scaled(W011[:, :, :], 1 / np.sqrt(FAN1))
                scaled(W101[:, :, :], 1 / np.sqrt(FAN1))
                scaled(L0[:, :], 1 / np.sqrt(M0))
                scaled(L1[:, :], 1 / np.sqrt(M1))
                act.wait_ge(s["rows_ready"], 3)
                with act.Fori(2, NSC // 2) as i:
                    for slot in range(2):
                        step(i * (2 * SC) + slot * SC, slot, i * (16 * SC))
                for t in range(NSC // 2 * 2, NSC):
                    step(t * SC, t % 2, 16 * SC * (t // 2))

            @block.tensor
            def _(pe):
                pe.wait_ge(s["consts_made"], 7)
                pe.wait_ge(s["counts_ready"], 1)
                pe.matmul(cps[:, 0, :], lower[:, :], cnt[:, :], start=True, stop=True)
                pe.matmul(cps[:, 1, :], ones[:, :], cnt[:, :], start=True, stop=True).then_inc(s["prefix_ready"], 1)
                pe.wait_ge(s["weights_scaled"], n_scaled[0])
                idn = ident[0:B, 0:B]
                with pe.Fori(0, NB) as b:
                    pe.wait_ge(hp["h_staged"], b + 1)
                    pe.transpose(psH[0:V, B:2 * B], hst[:, M0:D], idn)
                    pe.transpose(psH[0:M0, 0:B], hst[:, 0:M0], idn).then_inc(hp["h_transposed"], 1)
                    pe.wait_ge(hp["h_copied"], 2 * b + 2)
                    pe.wait_ge(hp["T011_staged"], b + 1)
                    for i in range(2):
                        last = pe.matmul(psT0[0:B, i, :], h0T[:, :],
                                         W011[:, i * 16:(i + 1) * 16, :].rearrange("p v w -> p (v w)"),
                                         start=True, stop=True)
                    last.then_inc(hp["T011_ready"], 1)
                    pe.wait_ge(hp["linear_added"], 2 * b + 2)
                    pe.matmul(psL[0:B, M0:D], h1T[:, :], L1[:, :], start=True, stop=True)
                    pe.matmul(psL[0:B, 0:M0], h0T[:, :], L0[:, :], start=True, stop=True
                              ).then_inc(hp["linear_ready"], 1)

            @block.vector
            def _(dve):
                n = [0]

                def link(ins):
                    n[0] += 1
                    ins.then_inc(s["v"], 1)
                    dve.wait_ge(s["v"], n[0])

                dve.wait_ge(s["edges_loaded"], 64)
                link(dve.tensor_copy(src_f[:, :], src_i[:, :]))
                link(dve.tensor_scalar(t1[:, :], src_f[:, :], 1.0 / B, 0.5 / B - 0.5, ALU.mult, ALU.add))
                link(dve.tensor_scalar(t2[:, :], t1[:, :], MAGIC, None, ALU.add))
                link(dve.tensor_scalar(blk[:, :], t2[:, :], -MAGIC, None, ALU.add))
                dve.sem_inc(s["blocks_ready"], 1)
                for b in range(NB + 1):
                    ins = dve.tensor_scalar(big[:, b, :], blk[:, :], float(b), 0.0, ALU.is_equal, ALU.add,
                                            accum_out=cnt[:, b:b + 1])
                    n[0] += 1
                    ins.then_inc(s["v"], 1)
                dve.wait_ge(s["v"], n[0])
                dve.sem_inc(s["counts_ready"], 1)
                dve.wait_ge(s["local_begun"], 1)
                link(dve.tensor_tensor(local[:, :], src_f[:, :], local[:, :], ALU.add))
                dve.wait_ge(s["prefix_ready"], 1)
                ceil0, ceil1, ngr, incl, first, base = (small[:, i, :] for i in range(6))
                link(dve.tensor_scalar(ceil0, cps[:, 1, :], 1.0 / GE, 0.5 - 0.5 / GE, ALU.mult, ALU.add))
                link(dve.tensor_scalar(ceil1, ceil0, MAGIC, None, ALU.add))
                link(dve.tensor_scalar(ngr, ceil1, -MAGIC, None, ALU.add))
                link(dve.memset(small[:, 6, :], 0.0))
                link(dve.tensor_tensor_scan(incl, ngr, small[:, 6, :], 0.0, ALU.add, ALU.add))
                link(dve.tensor_tensor(first, incl, ngr, ALU.subtract))
                link(dve.memset(first[:, NB:NB + 1], float(NG)))
                link(dve.scalar_tensor_tensor(base, first, float(GE), cps[:, 0, :], ALU.mult, ALU.add))

                def rank_columns(c0, c1, held):
                    w, cs = c1 - c0, slice(c0, c1)
                    places = scan[:, :, :].rearrange("p b t -> p (b t)")[:, 0:held * w].rearrange(
                        "p (b t) -> p b t", b=held)
                    for b0 in range(0, NB + 1, held):
                        for b in range(b0, b0 + held):
                            start = base if c0 == 0 else carry
                            ins = dve.tensor_tensor_scan(places[:, b - b0, :], big[:, b, cs], big[:, b, cs],
                                                         start[:, b:b + 1], ALU.add, ALU.bypass)
                            n[0] += 1
                            ins.then_inc(s["v"], 1)
                        dve.wait_ge(s["v"], n[0])
                        if c1 < EC:
                            link(dve.tensor_copy(carry[:, b0:b0 + held], places[:, :, w - 1]))
                        link(dve.tensor_tensor(big[:, b0:b0 + held, cs], big[:, b0:b0 + held, cs], places, ALU.mult))
                    link(dve.tensor_reduce(t2[:, cs], big[:, :, cs].rearrange("p b t -> p t b"), AX.X, ALU.add))
                    link(dve.tensor_scalar(src_f[:, cs], t2[:, cs], -1.0, None, ALU.add))
                    link(dve.tensor_scalar(t1[:, cs], src_f[:, cs], 1.0 / P, 0.5 / P - 0.5, ALU.mult, ALU.add))
                    link(dve.tensor_scalar(t2[:, cs], t1[:, cs], MAGIC, None, ALU.add))
                    link(dve.tensor_scalar(t1[:, cs], t2[:, cs], -MAGIC, None, ALU.add))
                    link(dve.scalar_tensor_tensor(t2[:, cs], t1[:, cs], -float(P), src_f[:, cs],
                                                  ALU.mult, ALU.add))
                    link(dve.scalar_tensor_tensor(row_f[:, cs], t2[:, cs], float(NT), t1[:, cs], ALU.mult, ALU.add))
                    link(dve.tensor_scalar(t1[:, cs], blk[:, cs], float(NB), None, ALU.is_equal))
                    link(dve.tensor_scalar(t2[:, cs], src_f[:, cs], float(DUMP - NG * GE), None, ALU.add))
                    link(dve.tensor_tensor(t2[:, cs], t2[:, cs], row_f[:, cs], ALU.subtract))
                    link(dve.tensor_tensor(t2[:, cs], t2[:, cs], t1[:, cs], ALU.mult))
                    link(dve.tensor_tensor(row_f[:, cs], row_f[:, cs], t2[:, cs], ALU.add))
                    dve.sem_inc(s["rows_ready"], 1)

                rank_columns(0, EARLY, NB + 1)
                rank_columns(EARLY, NEXT, NB + 1)
                rank_columns(NEXT, EC, HB)
                dve.wait_ge(s["nodes_loaded"], 16)
                xv = hx_sb[:, :, :]
                xc = big[0:B, :, :].rearrange("p b t -> p (b t)")[:, 0:NB * D].rearrange("p (b f) -> p b f", f=D)
                sq = scan[0:B, :, :].rearrange("p b t -> p (b t)")[:, 0:NB * D].rearrange("p (b f) -> p b f", f=D)

                def each(a):
                    return a.unsqueeze(2).broadcast_to([B, NB, D])
                link(dve.tensor_reduce(mv[:, 0, :], xv, AX.X, ALU.add))
                link(dve.tensor_scalar(mv[:, 0, :], mv[:, 0, :], 1.0 / D, None, ALU.mult))
                link(dve.tensor_tensor(xc, xv, each(mv[:, 0, :]), ALU.subtract))
                link(dve.tensor_tensor(sq, xc, xc, ALU.mult))
                link(dve.tensor_reduce(mv[:, 1, :], sq, AX.X, ALU.add))
                link(dve.tensor_scalar(mv[:, 1, :], mv[:, 1, :], 1.0 / D, 1e-5, ALU.mult, ALU.add))
                dve.sem_inc(s["var_ready"], 1)
                dve.wait_ge(s["std_ready"], 1)
                link(dve.reciprocal(mv[:, 2, :], mv[:, 3, :]))
                link(dve.tensor_tensor(sq, xc, each(mv[:, 2, :]), ALU.mult))
                link(dve.tensor_scalar(xc, sq, 0.0, None, ALU.max))
                dve.tensor_copy(h_sb[:, :, 0:M0], xc[:, :, 0:M0]).then_inc(s["h_ready"], 1)
                dve.tensor_copy(h_sb[:, :, M0:D].rearrange("p b (k u) -> p b u k", k=3),
                                xc[:, :, M0:D].rearrange("p b (u k) -> p b u k", k=3)).then_inc(s["h_ready"], 1)
                link(dve.tensor_tensor(hx_sb[:, :, :], xv, xc, ALU.add))
                gview = big[:, :, :].rearrange("p b t -> p (b t)")[:, 0:NB * NG].rearrange("p (b g) -> p g b", b=NB)
                link(dve.tensor_tensor(gview, gidx[:, :].unsqueeze(2).broadcast_to([P, NG, NB]),
                                       incl[:, None, 0:NB].broadcast_to([P, NG, NB]), ALU.is_ge))
                link(dve.tensor_reduce(gidx[:, :], gview, AX.X, ALU.add))
                link(dve.tensor_scalar(gblk_i[:, :], gidx[:, :], float(NB - 1), None, ALU.min))
                dve.sem_inc(hp["T011_staged"], 1)
                dve.sem_inc(hp["linear_added"], 2)
                dve.wait_ge(s["h_ready"], 2)
                with dve.Fori(0, NB) as b:
                    at = bass.ds(b, 1)
                    dve.tensor_copy(hst[:, None, :], h_sb[:, at, :]).then_inc(hp["h_staged"], 1)
                    dve.wait_ge(hp["h_transposed"], b + 1)
                    dve.wait_ge(hp["h0T_stored"], b * 16 + 16)
                    dve.tensor_copy(h0T[:, :], psH[0:M0, 0:B]).then_inc(hp["h_copied"], 1)
                    dve.tensor_copy(h1T[:, :], psH[0:V, B:2 * B]).then_inc(hp["h_copied"], 1)
                    dve.wait_ge(hp["T011_ready"], b + 1)
                    dve.wait_ge(hp["T011_stored"], b * 16 + 16)
                    dve.tensor_copy(tst, psT0[0:B, :, :].rearrange("p i f -> p (i f)")).then_inc(hp["T011_staged"], 1)
                    dve.wait_ge(hp["linear_ready"], b + 1)
                    dve.tensor_tensor(hx_sb[:, at, 0:M0], hx_sb[:, at, 0:M0], psL[0:B, None, 0:M0], ALU.add
                                      ).then_inc(hp["linear_added"], 1)
                    hx1 = hx_sb[:, at, M0:D].rearrange("p b (u k) -> p b u k", k=3)
                    dve.tensor_tensor(hx1, hx1, psL[0:B, None, M0:D].rearrange("p b (k u) -> p b u k", k=3), ALU.add
                                      ).then_inc(hp["linear_added"], 1)

        sums = ExitStack()
        rec = sums.enter_context(nc.sbuf_tensor("rec", [P, NSLOT, GT, REC], f32))
        Z = sums.enter_context(nc.sbuf_tensor("Z", [P, NSLOT, GT, GW], f32))
        O = sums.enter_context(nc.sbuf_tensor("O", [P, NSLOT, GT, B], f32))
        rv = sums.enter_context(nc.sbuf_tensor("rv", [P, 2, GT, 3, M1], f32))
        nodes = sums.enter_context(nc.sbuf_tensor("node_numbers", [P, B], f32))
        gp = sums.enter_context(nc.psum_tensor("G_part", [P, NPART, 2, 512], f32))
        q = {n: sem(n) for n in (
            "numbers_made", "G_added", "products", "edge_products", "G_part_ready",
            "rv_step", "gathers_begun")}
        rec_in = [sem(f"rec_in{i}") for i in range(NSLOT)]
        gathered = [sem(f"gathered{i}") for i in range(NSLOT)]
        LOOPS, LEFT = divmod(NG, NSLOT)
        assert LEFT >= AHEAD and NSLOT % NPART == 0
        rec_rows = rec_dram[0:P * NT, :].rearrange("(p t) c -> p t c", p=P)

        def groups(eng, body):
            with eng.Fori(0, LOOPS) as i:
                for slot in range(NSLOT):
                    body(i * NSLOT + slot, i, slot)
            for slot in range(LEFT):
                body(LOOPS * NSLOT + slot, LOOPS, slot)

        with sums, nc.Block() as block:

            @block.sync
            def _(sp):
                def load(g, turn, slot):
                    sp.wait_ge(q["G_part_ready"], g + 1)
                    sp.dma_start(rec[:, slot, :, :], rec_rows[:, bass.ds(g * GT, GT), :]).then_inc(rec_in[slot], 16)
                groups(sp, load)

            @block.gpsimd
            def _(pool):
                pool.iota(nodes[:, :], pattern=[[1, B]], base=1, channel_multiplier=0,
                          allow_small_or_imprecise_dtypes=True).then_inc(q["numbers_made"], 1)

                def gather(g, turn, slot):
                    pool.wait_ge(q["G_part_ready"], g + 1)
                    pool.wait_ge(rec_in[slot], turn * 16 + 16)
                    pool.sem_inc(q["gathers_begun"], 1)
                    for j in range(GT):
                        pool.indirect_dma_start(
                            Z[:, slot, j, 0:D], None, h_dram,
                            bass.IndirectOffsetOnAxis(ap=rec[:, slot, j, 1:2].bitcast(i32), axis=0)
                        ).then_inc(gathered[slot], 16)
                groups(pool, gather)

            @block.scalar
            def _(act):
                def scale_rows(g, turn, slot):
                    act.wait_ge(gathered[slot], turn * (16 * GT) + 16 * GT)
                    for j in range(GT):
                        act.activation(Z[:, slot, j, GD:GD + D], Z[:, slot, j, GH:GH + D], ACT.Copy,
                                       scale=rec[:, slot, j, 5:6]).then_inc(q["edge_products"], 1)
                        for k in range(1, 3):
                            lo = GR + k * M0
                            act.activation(Z[:, slot, j, lo:lo + M0], Z[:, slot, j, GH:GH + M0], ACT.Copy,
                                           scale=rec[:, slot, j, 2 + k:3 + k]).then_inc(q["edge_products"], 1)
                groups(act, scale_rows)

            @block.tensor
            def _(pe):
                pe.sem_inc(q["G_part_ready"], NSLOT)

                def product(g, turn, slot):
                    pe.wait_ge(q["products"], 3 * g + 3)
                    pe.wait_ge(q["edge_products"], 3 * GT * g + 3 * GT)
                    pe.wait_ge(q["G_added"], g + 1)
                    for j in range(GT):
                        for i in range(2):
                            last = pe.matmul(gp[0:B, slot % NPART, i, 0:HALF], O[:, slot, j, :],
                                             Z[:, slot, j, i * HALF:(i + 1) * HALF], start=j == 0, stop=j == GT - 1)
                    last.then_inc(q["G_part_ready"], 1)
                groups(pe, product)

            @block.vector
            def _(dve):
                dve.sem_inc(q["G_added"], NPART)
                dve.wait_ge(q["numbers_made"], 1)

                def add(g, slot, at):
                    dve.wait_ge(q["G_part_ready"], g + 1 + NSLOT)
                    dve.wait_ge(q["G_added"], g + NPART)
                    dve.tensor_tensor(G[0:B, bass.ds(at, 1), :, :], G[0:B, bass.ds(at, 1), :, :],
                                      gp[0:B, slot % NPART:slot % NPART + 1, :, 0:HALF], ALU.add).then_inc(q["G_added"], 1)

                def products(g, turn, slot):
                    c = rec[:, slot, :, :]
                    zs = Z[:, slot, :, :]
                    h = slot % 2
                    dve.wait_ge(rec_in[slot], turn * 16 + 16)
                    dve.wait_ge(q["G_part_ready"], g + 1)
                    dve.tensor_tensor(O[:, slot, :, :], nodes[:, None, :].broadcast_to([P, GT, B]),
                                      c[:, :, 0:1].broadcast_to([P, GT, B]), ALU.is_equal).then_inc(q["products"], 1)
                    dve.wait_ge(gathered[slot], turn * (16 * GT) + 16 * GT)
                    dve.tensor_tensor(rv[:, h, :, :, :], zs[:, :, M0:D].rearrange("p j (k u) -> p j k u", k=3),
                                      c[:, :, 2:5].unsqueeze(3).broadcast_to([P, GT, 3, M1]), ALU.mult
                                      ).then_inc(q["rv_step"], 1)
                    dve.tensor_tensor(zs[:, :, GR:GR + M0], zs[:, :, 0:M0], c[:, :, 2:3].broadcast_to([P, GT, M0]),
                                      ALU.mult).then_inc(q["products"], 1)
                    dve.wait_ge(q["rv_step"], g + 1)
                    dve.tensor_reduce(zs[:, :, GV:GW], rv[:, h, :, :, :].rearrange("p j k u -> p j u k"), AX.X, ALU.add
                                      ).then_inc(q["products"], 1)

                def block_numbers(g0, n):
                    return nc.values_load_multi_w_load_instructions(
                        gblk_i[0:1, bass.ds(g0, n)], engines=[mybir.EngineType.DVE], min_val=0, max_val=NB - 1)[1]

                for g in range(AHEAD):
                    products(g, 0, g)
                with dve.Fori(0, LOOPS) as i:
                    at = block_numbers(i * NSLOT, NSLOT)
                    for slot in range(NSLOT):
                        g = i * NSLOT + slot
                        products(g + AHEAD, i + (slot + AHEAD) // NSLOT, (slot + AHEAD) % NSLOT)
                        add(g, slot, at[slot])
                at = block_numbers(LOOPS * NSLOT, LEFT)
                for slot in range(LEFT):
                    if slot + AHEAD < LEFT:
                        products(LOOPS * NSLOT + slot + AHEAD, LOOPS, slot + AHEAD)
                    add(LOOPS * NSLOT + slot, slot, at[slot])

        up = ExitStack()

        def ub(name, shape):
            return up.enter_context(nc.sbuf_tensor(name, shape, f32))
        Gs = ub("Gs", [B, 2, GW])
        hs = ub("hs", [B, 2, D])
        GT_ = ub("GT", [P, 2, NCH, B])
        a_sb = ub("agg", [B, 2, D])
        a00 = ub("a00", [B, 2, 2, M0])
        a0T = ub("a0T", [P, 2, B])
        hb = ub("hb", [P, HC, B])
        pairsT = ub("pairsT", [P, 2, HC, B])
        t011 = ub("t011", [B, 2, M1, M1])
        pairs = ub("pairs", [B, 2, NTC * P])
        q3 = ub("q3", [B, 3, M1 * M1])
        PT = ub("PT", [P, 2, TQ, B])
        sumT = ub("sumT", [P, 2, B])
        fold = ub("fold", [P, M0])
        prod = ub("prod", [B, 3, 2, M1, M1])
        vsum = ub("vsum", [B, 2, 3, M1])
        res = ub("res", [B, 2, D])
        psA = up.enter_context(nc.psum_tensor("psA", [P, 2, 512], f32))
        psO = up.enter_context(nc.psum_tensor("psO", [P, 2, 512], f32))
        psT = up.enter_context(nc.psum_tensor("psT", [P, 2, 512], f32))
        psP = up.enter_context(nc.psum_tensor("psP", [P, 2, 512], f32))
        u = {n: sem(n) for n in (
            "block_staged", "preparing", "prepared", "T101_ready", "T101_used", "products_by_vector",
            "products_by_pool", "vsum_ready", "pairs_by_vector", "pairs_by_pool", "rows_paired", "pool_step",
            "chunks_transposed", "chunks_copied", "chunks_summed", "res_ready", "res_stored",
            "hb_in", "loads_begun", "fold_made", "sums_copied", "out0_ready",
            "first_rows_paired")}
        NPREP = 5
        out_v = out.rearrange("(b p) f -> p b f", p=B)

        AGG_AT, A0T_AT, T_AT, GT_AT = 0, 1, 2, 4
        VP = 18
        stored = [sem("stored0"), sem("stored1")]
        t011_in = [sem("t011_in0"), sem("t011_in1")]
        hs_in = [sem("hs_in0"), sem("hs_in1")]

        def pipelined(eng, step):
            loops = (NB - 2) // 2
            with eng.Fori(0, loops) as i:
                for slot in range(2):
                    step(i * 2 + slot, slot, i * 2 + slot + 1)
            for b in range(2 * loops, NB):
                step(b, b % 2, b + 1 if b + 1 < NB else None)

        def from_second(eng, step):
            step(0, 0)
            loops = (NB - 2) // 2
            with eng.Fori(0, loops) as i:
                for n in range(2):
                    step(i * 2 + n + 1, 1 - n)
            for b in range(2 * loops + 1, NB):
                step(b, b % 2)

        def has(b):
            return not isinstance(b, int) or b < NB

        def pairs_free(b):
            return 1 if isinstance(b, int) and b == 0 else b * NQ - NQ + 2

        def vectors(a, slot):
            return a[:, slot, M0:D].rearrange("p (k u) -> p k u", k=3)

        with up, nc.Block() as block:

            @block.scalar
            def _(act):
                act.sem_inc(u["chunks_copied"], 2)
                act.sem_inc(u["prepared"], 1)
                act.sem_inc(u["rows_paired"], VF)

                def stage(b, slot):
                    act.activation(Gs[:, slot, :], G[0:B, bass.ds(b, 1), :, :].rearrange("p b i f -> p (b i f)"),
                                   ACT.Copy).then_inc(u["block_staged"], 1)

                def prepare(b, slot, part):
                    act.wait_ge(u["preparing"], 3 * b + 1 + part)

                    def copy(dst, of):
                        act.activation(dst, of, ACT.Copy).then_inc(u["prepared"], 1)
                    if part == 0:
                        copy(GT_[:, slot, 0:4, :], psA[:, 0, 0:4 * B].rearrange("p (c n) -> p c n", c=4))
                        copy(GT_[0:GREST, slot, 4, :], psA[0:GREST, 1, 0:B])
                    elif part == 1:
                        copy(a_sb[:, slot, :], psA[0:B, 0, 0:D])
                        copy(a00[:, slot, :, :], psA[0:B, 0, None, 0:M0].broadcast_to([B, 2, M0]))
                    else:
                        copy(a0T[:, slot, :], psA[:, 1, 0:B])

                def pair(b, slot, r):
                    row = 2 * HC + r
                    act.activation(pairs[:, slot, r * M0:(r + 1) * M0], a_sb[:, slot, 0:M0], ACT.Copy,
                                   scale=hs[:, slot, row:row + 1]).then_inc(u["rows_paired"], 1)

                def all_pairs(b, slot, rows):
                    act.wait_ge(u["prepared"], NPREP * b + 4)
                    act.wait_ge(hs_in[slot], (b - slot) * 8 + 16)
                    for r in rows:
                        pair(b, slot, r)

                def step(b, slot, nxt):
                    for c in range(NQ):
                        act.wait_ge(u["chunks_transposed"], b * NQ + c + 1)
                        act.wait_ge(u["chunks_summed"], b * NQ + c + 1)
                        act.activation(PT[:, c % 2, :, :], psP[:, c % 2, 0:TQ * B].rearrange("p (c n) -> p c n", c=TQ),
                                       ACT.Copy).then_inc(u["chunks_copied"], 1)
                        if c == AGG_AT and nxt is not None:
                            prepare(nxt, 1 - slot, 1)
                        if c == A0T_AT and nxt is not None:
                            prepare(nxt, 1 - slot, 2)
                        if c == GT_AT - 1 and has(b + 2):
                            stage(b + 2, slot)
                        if c == GT_AT and has(b + 2):
                            prepare(b + 2, slot, 0)
                        if nxt is not None:
                            all_pairs(nxt, 1 - slot, range(VA * c // NQ, VA * (c + 1) // NQ))
                    act.wait_ge(u["chunks_summed"], b * NQ + NQ + 2)
                    act.activation(sumT[:, slot, :], psO[:, slot, 0:B], ACT.Copy).then_inc(u["sums_copied"], 1)

                for i in range(2):
                    half = slice(i * M0, (i + 1) * M0)
                    act.activation(fold[half, :], ident[half, half], ACT.Copy).then_inc(u["fold_made"], 1)
                stage(0, 0)
                for part in range(3):
                    prepare(0, 0, part)
                all_pairs(0, 0, range(VA - VF))
                stage(1, 1)
                prepare(1, 1, 0)
                pipelined(act, step)

            @block.tensor
            def _(pe):
                pe.sem_inc(u["chunks_summed"], 2)
                idn = ident[0:B, 0:B]

                def prepare(b, slot, part):
                    if part == 0:
                        pe.wait_ge(u["block_staged"], b + 1)
                        pe.wait_ge(u["prepared"], NPREP * b + 1)
                        for c in range(4):
                            pe.transpose(psA[:, 0, c * B:(c + 1) * B], Gs[:, slot, c * P:(c + 1) * P], idn)
                        last = pe.transpose(psA[0:GREST, 1, 0:B], Gs[:, slot, 4 * P:GW], idn)
                    elif part == 1:
                        pe.wait_ge(u["prepared"], NPREP * b + 3)
                        for c in range(NCH):
                            k = P if c < NCH - 1 else GREST
                            last = pe.matmul(psA[0:B, 0, 0:D], GT_[0:k, slot, c, :], Wm[0:k, c, :],
                                             start=c == 0, stop=c == NCH - 1)
                    else:
                        pe.wait_ge(u["prepared"], NPREP * b + 5)
                        last = pe.transpose(psA[:, 1, 0:B], a00[:, slot, :, :].rearrange("p i v -> p (i v)"), idn)
                    last.then_inc(u["preparing"], 1)

                def first_products(b, slot):
                    pe.wait_ge(u["T101_used"], b + 1)
                    pe.wait_ge(u["prepared"], NPREP * b + 6)
                    for i in range(2):
                        last = pe.matmul(psT[0:B, i, :], a0T[0:M0, slot, :],
                                         W101[:, i * 16:(i + 1) * 16, :].rearrange("p u w -> p (u w)"),
                                         start=True, stop=True)
                    last.then_inc(u["T101_ready"], 1)

                def fold_sums(b, slot):
                    pe.wait_ge(u["sums_copied"], b + 1)
                    pe.matmul(psO[0:B, slot, P:P + M0], sumT[:, slot, :], fold[:, :], start=True, stop=True
                              ).then_inc(u["out0_ready"], 1)

                def step(b, slot):
                    nxt = b + 1 if has(b + 1) else None
                    pe.wait_ge(u["pairs_by_vector"], b + 1)
                    pe.wait_ge(u["res_ready"], 2 * b + 1)
                    chunks = iter(range(NC))

                    def sum_chunk(pairs_T, ch):
                        turn = next(chunks)
                        half = slice(turn % 2 * M0, (turn % 2 + 1) * M0)
                        return pe.matmul(psO[half, slot, 0:B], W0[:, ch, :], pairs_T,
                                         start=turn < 2, stop=turn >= NC - 2)

                    for c in range(NQ + 1):
                        if c < NQ:
                            pe.wait_ge(u["chunks_copied"], b * NQ + c + 1)
                            if isinstance(b, int) and b == 0 and 2 * TQ * c < VA:
                                if 2 * TQ * c < VA - VF:
                                    pe.wait_ge(u["rows_paired"], VF + 2 * TQ * (c + 1))
                                else:
                                    pe.wait_ge(u["first_rows_paired"], 1)
                            elif 2 * TQ * c < VA:
                                pe.wait_ge(u["rows_paired"], VA * b + 2 * TQ * (c + 1))
                            else:
                                pe.wait_ge(u["pairs_by_pool"], b + 2)
                            for m in range(TQ):
                                ch = c * TQ + m
                                last = pe.transpose(psP[:, c % 2, m * B:(m + 1) * B],
                                                    pairs[:, slot, ch * P:(ch + 1) * P], idn)
                            last.then_inc(u["chunks_transposed"], 1)
                        if c == AGG_AT and nxt is not None:
                            prepare(nxt, 1 - slot, 1)
                        if c == A0T_AT and nxt is not None:
                            prepare(nxt, 1 - slot, 2)
                        if c == GT_AT and has(b + 2):
                            prepare(b + 2, slot, 0)
                        if nxt is not None and c == T_AT:
                            first_products(nxt, 1 - slot)
                        for ch in range(HC * c // (NQ + 1), HC * (c + 1) // (NQ + 1)):
                            sum_chunk(pairsT[:, slot, ch, :], ch)
                        if c == 1 and (not isinstance(b, int) or b > 0):
                            fold_sums(b - 1, 1 - slot)
                        if c > 0:
                            pe.wait_ge(u["chunks_copied"], b * NQ + c + 2)
                            for m in range(TQ):
                                last = sum_chunk(PT[:, (c - 1) % 2, m, :], HC + (c - 1) * TQ + m)
                            last.then_inc(u["chunks_summed"], 1)

                for part in range(3):
                    prepare(0, 0, part)
                first_products(0, 0)
                prepare(1, 1, 0)
                pe.wait_ge(u["fold_made"], 2)
                from_second(pe, step)
                fold_sums(NB - 1, (NB - 1) % 2)

            @block.gpsimd
            def _(pool):
                pool.sem_inc(u["pairs_by_pool"], 1)

                def make_pairs(b, slot):
                    pool.wait_ge(u["prepared"], NPREP * b + 4)
                    pool.wait_ge(hs_in[slot], (b - slot) * 8 + 16)
                    pool.wait_ge(u["pairs_by_pool"], b + 1)
                    a, h = a_sb[:, slot, :], hs[:, slot, :]
                    for k in range(3):
                        lo = M0 + k * M1
                        pool.tensor_tensor(q3[:, k, :].rearrange("p (u v) -> p u v", v=M1),
                                           h[:, lo:lo + M1].unsqueeze(2).broadcast_to([B, M1, M1]),
                                           a[:, None, lo:lo + M1].broadcast_to([B, M1, M1]), ALU.mult
                                           ).then_inc(u["pool_step"], 1)

                def sum_pairs(b, slot):
                    pool.wait_ge(u["pool_step"], 4 * b + 3)
                    pool.tensor_tensor(q3[:, 0, :], q3[:, 0, :], q3[:, 1, :], ALU.add).then_inc(u["pool_step"], 1)
                    pool.wait_ge(u["pool_step"], 4 * b + 4)
                    pool.wait_ge(u["chunks_summed"], pairs_free(b))
                    pool.tensor_tensor(pairs[:, slot, VA * M0:NTC * P], q3[:, 0, :], q3[:, 2, :], ALU.add
                                       ).then_inc(u["pairs_by_pool"], 1)

                def products(b, slot):
                    pool.wait_ge(t011_in[slot], (b - slot) * 8 + 16)
                    pool.wait_ge(u["vsum_ready"], b + 1)
                    pool.tensor_tensor(prod[:, :, 0, 0:VP, :], t011[:, slot, None, 0:VP, :].broadcast_to([B, 3, VP, M1]),
                                       vectors(a_sb, slot)[:, :, 0:VP].unsqueeze(3).broadcast_to([B, 3, VP, M1]),
                                       ALU.mult).then_inc(u["products_by_pool"], 1)

                def block_work(b, slot):
                    make_pairs(b, slot)
                    products(b, slot)
                    sum_pairs(b, slot)

                def step(b, slot, nxt):
                    if nxt is not None:
                        block_work(nxt, 1 - slot)
                block_work(0, 0)
                pipelined(pool, step)

            @block.vector
            def _(dve):
                dve.sem_inc(u["T101_used"], 1)
                dve.sem_inc(u["res_ready"], 4)
                dve.sem_inc(u["vsum_ready"], 1)

                def make_pairs(b, slot):
                    dve.wait_ge(u["prepared"], NPREP * b + 6)
                    dve.wait_ge(u["hb_in"], b * 32 + 32)
                    dve.wait_ge(u["chunks_summed"], pairs_free(b))
                    dve.tensor_tensor(pairsT[:, slot, :, :], hb[:, :, :], a0T[:, slot, None, :].broadcast_to([P, HC, B]),
                                      ALU.mult).then_inc(u["pairs_by_vector"], 1)

                def second_products(b, slot):
                    dve.wait_ge(u["T101_ready"], b + 1)
                    dve.wait_ge(hs_in[slot], (b - slot) * 8 + 16)
                    dve.wait_ge(u["vsum_ready"], b + 1)
                    dve.tensor_tensor(
                        prod[:, :, 1, :, :],
                        psT[0:B, :, :].rearrange("p i (c w) -> p (i c) w", w=M1)[:, None, :, :].broadcast_to(
                            [B, 3, M1, M1]),
                        vectors(hs, slot).unsqueeze(3).broadcast_to([B, 3, M1, M1]), ALU.mult
                    ).then_inc(u["T101_used"], 1)
                    dve.wait_ge(t011_in[slot], (b - slot) * 8 + 16)
                    n = M1 - VP
                    dve.tensor_tensor(prod[:, :, 0, VP:M1, :],
                                      t011[:, slot, None, VP:M1, :].broadcast_to([B, 3, n, M1]),
                                      vectors(a_sb, slot)[:, :, VP:M1].unsqueeze(3).broadcast_to([B, 3, n, M1]),
                                      ALU.mult).then_inc(u["products_by_vector"], 1)

                def vector_sums(b, slot):
                    dve.wait_ge(u["T101_used"], b + 2)
                    dve.wait_ge(u["products_by_vector"], b + 1)
                    dve.wait_ge(u["products_by_pool"], b + 1)
                    dve.tensor_reduce(vsum[:, slot, :, :], prod[:, :, :, :, :].rearrange("p k i c w -> p k w (i c)"),
                                      AX.X, ALU.add).then_inc(u["vsum_ready"], 1)

                def finish(b, slot):
                    at = bass.ds(b, 1)
                    dve.wait_ge(u["out0_ready"], b + 1)
                    dve.wait_ge(u["res_stored"], b + 1)
                    dve.wait_ge(u["vsum_ready"], b + 2)
                    dve.tensor_tensor(res[:, slot, None, 0:M0], psO[0:B, slot, None, P:P + M0], hx_sb[:, at, 0:M0], ALU.add
                                      ).then_inc(u["res_ready"], 1)
                    dve.tensor_tensor(res[:, slot, None, M0:D].rearrange("p b (u k) -> p b u k", k=3),
                                      vsum[:, slot, :, :].rearrange("p k u -> p u k")[:, None, :, :],
                                      hx_sb[:, at, M0:D].rearrange("p b (u k) -> p b u k", k=3), ALU.add
                                      ).then_inc(u["res_ready"], 1)

                def step(b, slot):
                    second_products(b, slot)
                    if isinstance(b, int) and b == NB - 1:
                        finish(b - 1, 1 - slot)
                        vector_sums(b, slot)
                        return
                    vector_sums(b, slot)
                    if not isinstance(b, int) or b > 0:
                        finish(b - 1, 1 - slot)
                    make_pairs(b + 1, 1 - slot)

                make_pairs(0, 0)
                dve.wait_ge(hs_in[0], 16)
                dve.tensor_tensor(pairs[:, 0, (VA - VF) * M0:VA * M0].rearrange("p (u v) -> p u v", v=M0),
                                  hs[:, 0, M0 - VF:M0].unsqueeze(2).broadcast_to([B, VF, M0]),
                                  a_sb[:, 0, None, 0:M0].broadcast_to([B, VF, M0]), ALU.mult
                                  ).then_inc(u["first_rows_paired"], 1)
                from_second(dve, step)
                finish(NB - 1, (NB - 1) % 2)

            @block.sync
            def _(sp):
                sp.sem_inc(u["res_stored"], 2)

                def load_hb(b):
                    for i in range(2):
                        rows = h0t_dram[bass.ds(b, 1), i * HC:(i + 1) * HC, :].rearrange("b u n -> b (u n)")
                        sp.dma_start(hb[i * M0:(i + 1) * M0, :, :].rearrange("p u n -> p (u n)")[:, None, :],
                                     rows[None, :, :].broadcast_to([M0, 1, HC * B])).then_inc(u["hb_in"], 16)

                def load_h(b, slot):
                    sp.dma_start(hs[:, slot, None, :], h_dram.rearrange("(b p) f -> p b f", p=B)[:, bass.ds(b, 1), :]
                                 ).then_inc(hs_in[slot], 16)

                def load_t011(b, slot):
                    sp.dma_start(t011[:, slot, :, :].rearrange("p v w -> p (v w)")[:, None, :],
                                 t011_dram[bass.ds(b, 1), :, :].rearrange("b p f -> p b f")
                                 ).then_inc(t011_in[slot], 16)

                def step(b, slot, nxt):
                    if has(b + 2):
                        sp.wait_ge(u["pairs_by_vector"], b + 2)
                        sp.sem_inc(u["loads_begun"], 1)
                        load_hb(b + 2)
                        sp.wait_ge(u["rows_paired"], b * VA + VA)
                        sp.sem_inc(u["loads_begun"], 1)
                        sp.wait_ge(u["pairs_by_pool"], b + 2)
                        sp.sem_inc(u["loads_begun"], 1)
                        sp.wait_ge(u["T101_used"], b + 2)
                        sp.sem_inc(u["loads_begun"], 1)
                        sp.wait_ge(u["products_by_pool"], b + 1)
                        sp.wait_ge(u["products_by_vector"], b + 1)
                        sp.sem_inc(u["loads_begun"], 1)
                        load_h(b + 2, slot)
                        load_t011(b + 2, slot)
                    sp.wait_ge(u["res_ready"], 2 * b + 6)
                    sp.dma_start(out_v[:, bass.ds(b, 1), :], res[:, slot, None, :]).then_inc(stored[slot], 16)
                    sp.wait_ge(stored[slot], (b - slot) * 8 + 16)
                    sp.sem_inc(u["res_stored"], 1)
                load_h(0, 0)
                load_hb(0)
                load_t011(0, 0)
                load_h(1, 1)
                load_t011(1, 1)
                sp.wait_ge(u["pairs_by_vector"], 1)
                load_hb(1)
                pipelined(sp, step)
                sp.wait_ge(stored[0], 16 * ((NB + 1) // 2))
                sp.wait_ge(stored[1], 16 * (NB // 2))


_INS = ["x", "src", "dst", "edge_attr_4"] + ["L0_gnn_" + n for n in (
    "wm000", "wm011", "wm101", "wm110", "lm0", "lm1", "wu000", "wu011", "wu101", "wu110", "lu0", "lu1")]


def kernel(**inputs):
    import concourse.bacc as _bacc
    from concourse.bass_utils import run_bass_kernel_spmd as _run

    nc = _bacc.Bacc("TRN2", target_bir_lowering=False, num_devices=1)
    arrays, args = {}, []
    for name in _INS:
        a = np.ascontiguousarray(inputs[name])
        arrays[f"in_{name}"] = a
        args.append(nc.dram_tensor(f"in_{name}", a.shape, mybir.dt.from_np(a.dtype), kind="ExternalInput").ap())
    shape = arrays["in_x"].shape
    args.append(nc.dram_tensor("out", shape, mybir.dt.float32, kind="ExternalOutput").ap())
    gnn_layer(nc, *args)
    r = _run(nc, [arrays], core_ids=[0])
    return r.results[0]["out"]
```
